# Optimizing a Trainium2 kernel written in Bass

```python
import numpy as np
import jax
import jax.numpy as jnp

def _softmax(x, axis=-1):
    return jax.nn.softmax(x, axis=axis)

def _gelu(x):
    return jax.nn.gelu(x, approximate=True)

def _silu(x):
    return jax.nn.silu(x)

def _sigmoid(x):
    return jax.nn.sigmoid(x)

def _layernorm(x, axis=-1, eps=1e-05):
    m = jnp.mean(x, axis=axis, keepdims=True)
    v = jnp.var(x, axis=axis, keepdims=True)
    return (x - m) / jnp.sqrt(v + eps)

def _scatter_add(tgt, idx, src, axis=0):
    return tgt.at[idx].add(src)

def _segment_sum(src, seg, n):
    return jax.ops.segment_sum(src, seg, n)
kernel_name = 'mk_hybrid_d1_jaxref_r8_04311a'

def setup_inputs(seed: int=0):
    np.random.seed(seed)
    _w = jnp.asarray

    def _L0_attn_a_setup():
        import jax, jax.numpy as jnp
        import numpy as np
        import math
        DIM = 128
        NUM_HEADS = 16
        HEAD_DIM = DIM // NUM_HEADS

        def build_rope_matrix(dim, seq_len):
            position = jnp.arange(seq_len, dtype=jnp.float32)[:, None]
            dim_pair = jnp.arange(0, dim, 2, dtype=jnp.float32)[None, :]
            theta = 10000.0 ** (-dim_pair / dim)
            freqs = position * theta
            return jnp.concatenate([jnp.cos(freqs), jnp.sin(freqs)], axis=-1)

        def apply_rope(x, rope):
            x1, x2 = (x[..., ::2], x[..., 1::2])
            cos = rope[..., ::2]
            sin = rope[..., 1::2]
            return jnp.concatenate([x1 * cos - x2 * sin, x1 * sin + x2 * cos], axis=-1)
        key = jax.random.key(seed)
        ks = jax.random.split(key, 9)
        B, N = (2, 256)
        x = jax.random.normal(ks[0], (B, N, DIM), dtype=jnp.float32)
        bound = math.sqrt(6.0 / (DIM + DIM))

        def w(k):
            return jax.random.uniform(k, (DIM, DIM), jnp.float32, -bound, bound)

        def b(k):
            return jax.random.uniform(k, (DIM,), jnp.float32, -1.0 / math.sqrt(DIM), 1.0 / math.sqrt(DIM))
        return {'x': x, 'Wq': w(ks[1]), 'bq': b(ks[2]), 'Wk': w(ks[3]), 'bk': b(ks[4]), 'Wv': w(ks[5]), 'bv': b(ks[6]), 'Wo': w(ks[7]), 'bo': b(ks[8])}
    _L0_attn_a_in = _L0_attn_a_setup()

    def _L0_attn_b_setup():
        import jax, jax.numpy as jnp
        import numpy as np
        B, S, E = (8, 128, 128)
        H = 16
        D = E // H

        def _split_heads(t, b, s):
            return t.reshape(b, s, H, D).transpose(0, 2, 1, 3)
        key = jax.random.key(seed)
        ks = jax.random.split(key, 5)
        scale = 1.0 / np.sqrt(E)
        return {'x': jax.random.normal(ks[0], (B, S, E), dtype=jnp.float32), 'Wq': jax.random.normal(ks[1], (E, E), dtype=jnp.float32) * scale, 'Wk': jax.random.normal(ks[2], (E, E), dtype=jnp.float32) * scale, 'Wv': jax.random.normal(ks[3], (E, E), dtype=jnp.float32) * scale, 'Wo': jax.random.normal(ks[4], (E, E), dtype=jnp.float32) * scale}
    _L0_attn_b_in = _L0_attn_b_setup()

    def _L0_ffn_setup():
        import jax, jax.numpy as jnp
        import numpy as np
        from jax import lax
        N_HEADS = 16
        TOP_K = 2
        N_EXPERTS = 8

        def layer_norm(x, w, b, eps=1e-05):
            mu = jnp.mean(x, axis=-1, keepdims=True)
            var = jnp.mean(jnp.square(x - mu), axis=-1, keepdims=True)
            return (x - mu) * lax.rsqrt(var + eps) * w + b

        def attention(x, w_qkv, b_qkv, w_o, b_o):
            B, T, D = x.shape
            dh = D // N_HEADS
            qkv = x @ w_qkv + b_qkv
            q, k, v = jnp.split(qkv, 3, axis=-1)
            q = q.reshape(B, T, N_HEADS, dh)
            k = k.reshape(B, T, N_HEADS, dh)
            v = v.reshape(B, T, N_HEADS, dh)
            scores = jnp.einsum('bqhd,bkhd->bhqk', q, k) / jnp.sqrt(jnp.float32(dh)).astype(x.dtype)
            probs = jax.nn.softmax(scores, axis=-1)
            ctx = jnp.einsum('bhqk,bkhd->bqhd', probs, v).reshape(B, T, D)
            return ctx @ w_o + b_o

        def moe_ff(x, w_gate, w1, b1, w2, b2):
            B, T, D = x.shape
            t = x.reshape(B * T, D)
            probs = jax.nn.softmax(t @ w_gate, axis=-1)
            tw, ti = lax.top_k(probs, TOP_K)
            tw = tw / jnp.sum(tw, axis=-1, keepdims=True)
            out = jnp.zeros_like(t)
            for e in range(N_EXPERTS):
                we = jnp.sum(jnp.where(ti == e, tw, 0.0), axis=-1)
                h = jax.nn.gelu(t @ w1[e] + b1[e]) @ w2[e] + b2[e]
                out = out + we[:, None] * h
            return out.reshape(B, T, D)
        key = jax.random.key(seed)
        ks = jax.random.split(key, 8)
        B, T, D, H, E = (4, 64, 128, 512, 8)
        s = lambda d: 1.0 / np.sqrt(d)
        return {'x': jax.random.normal(ks[0], (B, T, D), jnp.float32), 'ln1_w': jnp.ones((D,), jnp.float32), 'ln1_b': jnp.zeros((D,), jnp.float32), 'ln2_w': jnp.ones((D,), jnp.float32), 'ln2_b': jnp.zeros((D,), jnp.float32), 'w_qkv': jax.random.normal(ks[1], (D, 3 * D), jnp.float32) * s(D), 'b_qkv': jnp.zeros((3 * D,), jnp.float32), 'w_o': jax.random.normal(ks[2], (D, D), jnp.float32) * s(D), 'b_o': jnp.zeros((D,), jnp.float32), 'w_gate': jax.random.normal(ks[3], (D, E), jnp.float32) * s(D), 'w1': jax.random.normal(ks[4], (E, D, H), jnp.float32) * s(D), 'b1': jnp.zeros((E, H), jnp.float32), 'w2': jax.random.normal(ks[5], (E, H, D), jnp.float32) * s(H), 'b2': jnp.zeros((E, D), jnp.float32)}
    _L0_ffn_in = _L0_ffn_setup()
    _d = {'L0_attn_a_x': _L0_attn_a_in['x'], 'L0_attn_a_Wq': _L0_attn_a_in['Wq'], 'L0_attn_a_bq': _L0_attn_a_in['bq'], 'L0_attn_a_Wk': _L0_attn_a_in['Wk'], 'L0_attn_a_bk': _L0_attn_a_in['bk'], 'L0_attn_a_Wv': _L0_attn_a_in['Wv'], 'L0_attn_a_bv': _L0_attn_a_in['bv'], 'L0_attn_a_Wo': _L0_attn_a_in['Wo'], 'L0_attn_a_bo': _L0_attn_a_in['bo'], 'L0_attn_b_Wq': _L0_attn_b_in['Wq'], 'L0_attn_b_Wk': _L0_attn_b_in['Wk'], 'L0_attn_b_Wv': _L0_attn_b_in['Wv'], 'L0_attn_b_Wo': _L0_attn_b_in['Wo'], 'L0_ffn_ln1_w': _L0_ffn_in['ln1_w'], 'L0_ffn_ln1_b': _L0_ffn_in['ln1_b'], 'L0_ffn_ln2_w': _L0_ffn_in['ln2_w'], 'L0_ffn_ln2_b': _L0_ffn_in['ln2_b'], 'L0_ffn_w_qkv': _L0_ffn_in['w_qkv'], 'L0_ffn_b_qkv': _L0_ffn_in['b_qkv'], 'L0_ffn_w_o': _L0_ffn_in['w_o'], 'L0_ffn_b_o': _L0_ffn_in['b_o'], 'L0_ffn_w_gate': _L0_ffn_in['w_gate'], 'L0_ffn_w1': _L0_ffn_in['w1'], 'L0_ffn_b1': _L0_ffn_in['b1'], 'L0_ffn_w2': _L0_ffn_in['w2'], 'L0_ffn_b2': _L0_ffn_in['b2']}
    _x0 = _d['L0_attn_a_x']
    _d['L0_attn_a_x'] = jax.random.normal(jax.random.fold_in(jax.random.key(seed), 1), (8, 256, 128), dtype=_x0.dtype)
    del _x0
    return _d

def reference(L0_attn_a_x, L0_attn_a_Wq, L0_attn_a_bq, L0_attn_a_Wk, L0_attn_a_bk, L0_attn_a_Wv, L0_attn_a_bv, L0_attn_a_Wo, L0_attn_a_bo, L0_attn_b_Wq, L0_attn_b_Wk, L0_attn_b_Wv, L0_attn_b_Wo, L0_ffn_ln1_w, L0_ffn_ln1_b, L0_ffn_ln2_w, L0_ffn_ln2_b, L0_ffn_w_qkv, L0_ffn_b_qkv, L0_ffn_w_o, L0_ffn_b_o, L0_ffn_w_gate, L0_ffn_w1, L0_ffn_b1, L0_ffn_w2, L0_ffn_b2):

    def _L0_attn_a_ref(x, Wq, bq, Wk, bk, Wv, bv, Wo, bo):
        import jax, jax.numpy as jnp
        import numpy as np
        import math
        DIM = 128
        NUM_HEADS = 16
        HEAD_DIM = DIM // NUM_HEADS

        def build_rope_matrix(dim, seq_len):
            position = jnp.arange(seq_len, dtype=jnp.float32)[:, None]
            dim_pair = jnp.arange(0, dim, 2, dtype=jnp.float32)[None, :]
            theta = 10000.0 ** (-dim_pair / dim)
            freqs = position * theta
            return jnp.concatenate([jnp.cos(freqs), jnp.sin(freqs)], axis=-1)

        def apply_rope(x, rope):
            x1, x2 = (x[..., ::2], x[..., 1::2])
            cos = rope[..., ::2]
            sin = rope[..., 1::2]
            return jnp.concatenate([x1 * cos - x2 * sin, x1 * sin + x2 * cos], axis=-1)
        B, N, _ = x.shape
        H, hd = (NUM_HEADS, HEAD_DIM)
        rope = build_rope_matrix(hd, N)

        def proj(W, bias):
            y = x @ W.T + bias
            return y.reshape(B, N, H, hd).transpose(0, 2, 1, 3)
        q = apply_rope(proj(Wq, bq), rope)
        k = apply_rope(proj(Wk, bk), rope)
        v = apply_rope(proj(Wv, bv), rope)
        scores = jnp.einsum('bhqd,bhkd->bhqk', q, k) / math.sqrt(hd)
        probs = jax.nn.softmax(scores, axis=-1)
        out = jnp.einsum('bhqk,bhkd->bhqd', probs, v)
        out = apply_rope(out, -rope)
        out = out.transpose(0, 2, 1, 3).reshape(B, N, DIM)
        return out @ Wo.T + bo

    def _L0_attn_b_ref(x, Wq, Wk, Wv, Wo):
        import jax, jax.numpy as jnp
        import numpy as np
        B, S, E = (8, 128, 128)
        H = 16
        D = E // H

        def _split_heads(t, b, s):
            return t.reshape(b, s, H, D).transpose(0, 2, 1, 3)
        b, s, e = x.shape
        q = _split_heads(x @ Wq.T, b, s)
        k = _split_heads(x @ Wk.T, b, s)
        v = _split_heads(x @ Wv.T, b, s)
        d = q.shape[-1]
        q_c = q - q.mean(axis=-1, keepdims=True)
        k_c = k - k.mean(axis=-1, keepdims=True)
        cov = jnp.einsum('bhqd,bhkd->bhqk', q_c, k_c) / d
        q_var = (q_c * q_c).sum(axis=-1, keepdims=True) / (d - 1)
        k_var = (k_c * k_c).sum(axis=-1, keepdims=True) / (d - 1)
        var = jnp.einsum('bhqo,bhko->bhqk', q_var, k_var) / d
        attn = jax.nn.softmax(cov + var, axis=-1)
        out = jnp.einsum('bhqk,bhkd->bhqd', attn, v)
        out = out.transpose(0, 2, 1, 3).reshape(b, s, e)
        return out @ Wo.T

    def _L0_ffn_ref(x, ln1_w, ln1_b, ln2_w, ln2_b, w_qkv, b_qkv, w_o, b_o, w_gate, w1, b1, w2, b2):
        import jax, jax.numpy as jnp
        import numpy as np
        from jax import lax
        N_HEADS = 16
        TOP_K = 2
        N_EXPERTS = 8

        def layer_norm(x, w, b, eps=1e-05):
            mu = jnp.mean(x, axis=-1, keepdims=True)
            var = jnp.mean(jnp.square(x - mu), axis=-1, keepdims=True)
            return (x - mu) * lax.rsqrt(var + eps) * w + b

        def attention(x, w_qkv, b_qkv, w_o, b_o):
            B, T, D = x.shape
            dh = D // N_HEADS
            qkv = x @ w_qkv + b_qkv
            q, k, v = jnp.split(qkv, 3, axis=-1)
            q = q.reshape(B, T, N_HEADS, dh)
            k = k.reshape(B, T, N_HEADS, dh)
            v = v.reshape(B, T, N_HEADS, dh)
            scores = jnp.einsum('bqhd,bkhd->bhqk', q, k) / jnp.sqrt(jnp.float32(dh)).astype(x.dtype)
            probs = jax.nn.softmax(scores, axis=-1)
            ctx = jnp.einsum('bhqk,bkhd->bqhd', probs, v).reshape(B, T, D)
            return ctx @ w_o + b_o

        def moe_ff(x, w_gate, w1, b1, w2, b2):
            B, T, D = x.shape
            t = x.reshape(B * T, D)
            probs = jax.nn.softmax(t @ w_gate, axis=-1)
            tw, ti = lax.top_k(probs, TOP_K)
            tw = tw / jnp.sum(tw, axis=-1, keepdims=True)
            out = jnp.zeros_like(t)
            for e in range(N_EXPERTS):
                we = jnp.sum(jnp.where(ti == e, tw, 0.0), axis=-1)
                h = jax.nn.gelu(t @ w1[e] + b1[e]) @ w2[e] + b2[e]
                out = out + we[:, None] * h
            return out.reshape(B, T, D)
        h = x + attention(layer_norm(x, ln1_w, ln1_b), w_qkv, b_qkv, w_o, b_o)
        return h + moe_ff(layer_norm(h, ln2_w, ln2_b), w_gate, w1, b1, w2, b2)
    x = L0_attn_a_x
    x = x + _L0_attn_a_ref(_layernorm(x, axis=-1), L0_attn_a_Wq, L0_attn_a_bq, L0_attn_a_Wk, L0_attn_a_bk, L0_attn_a_Wv, L0_attn_a_bv, L0_attn_a_Wo, L0_attn_a_bo)
    x = x + _L0_ffn_ref(_layernorm(x, axis=-1), L0_ffn_ln1_w, L0_ffn_ln1_b, L0_ffn_ln2_w, L0_ffn_ln2_b, L0_ffn_w_qkv, L0_ffn_b_qkv, L0_ffn_w_o, L0_ffn_b_o, L0_ffn_w_gate, L0_ffn_w1, L0_ffn_b1, L0_ffn_w2, L0_ffn_b2)
    x = x + _L0_attn_b_ref(_layernorm(x, axis=-1), L0_attn_b_Wq, L0_attn_b_Wk, L0_attn_b_Wv, L0_attn_b_Wo)
    x = x + _L0_ffn_ref(_layernorm(x, axis=-1), L0_ffn_ln1_w, L0_ffn_ln1_b, L0_ffn_ln2_w, L0_ffn_ln2_b, L0_ffn_w_qkv, L0_ffn_b_qkv, L0_ffn_w_o, L0_ffn_b_o, L0_ffn_w_gate, L0_ffn_w1, L0_ffn_b1, L0_ffn_w2, L0_ffn_b2)
    return x

_drawn_inputs = setup_inputs


def setup_inputs(seed=0):
    import zlib

    import numpy as np

    out = dict(_drawn_inputs(seed))
    spreads = {'L0_ffn_ln1_w': (1.0, 0.2),
     'L0_ffn_ln1_b': (0.0, 0.1),
     'L0_ffn_ln2_w': (1.0, 0.2),
     'L0_ffn_ln2_b': (0.0, 0.1),
     'L0_ffn_b_qkv': (0.0, 0.1),
     'L0_ffn_b_o': (0.0, 0.1),
     'L0_ffn_b1': (0.0, 0.1),
     'L0_ffn_b2': (0.0, 0.1)}
    factors = {'L0_attn_a_bq': 2.888, 'L0_attn_a_bk': 3.602}
    for name, (base, spread) in spreads.items():
        noise = np.random.default_rng([zlib.crc32(name.encode()), seed]).standard_normal(out[name].shape)
        drawn = base * np.exp(spread * noise) if base else spread * noise
        out[name] = jnp.asarray(drawn.astype(out[name].dtype))
    for name, factor in factors.items():
        out[name] = (out[name] * factor).astype(out[name].dtype)
    return out
```

```python
import concourse.bass as bass
from concourse import mybir
from contextlib import ExitStack

F32 = mybir.dt.float32
F32R = mybir.dt.float32r
U32 = mybir.dt.uint32
ALU = mybir.AluOpType
ACT = mybir.ActivationFunctionType
AX = mybir.AxisListType

P = 128
D = 128
NB = 8
T = 256
TT = T // P
NT = NB * TT
H = 16
HD = D // H
SL = 32
HG = P // SL
NG = H // HG
SHIFT = 27
E = 8
FF = 512
FC = FF // P
BLK = 512
NBLK = NB * T // BLK
BT = BLK // P
EPS = 1e-5
SCALE = float(HD) ** -0.5
LAYERS = ["rope", "ffn", "cov", "ffn"]
EXP_SCALE = {"rope": SCALE, "ffn": SCALE, "cov": 1.0 / HD}


class Event:

    def __init__(self, sem, per):
        self.sem = sem
        self.per = per if isinstance(per, dict) else {k: per for k in LAYERS}

    def value(self, layer, b, k):
        per = self.per.get(LAYERS[layer], 0)
        k = per if k is None else k
        const = sum(NB * self.per.get(LAYERS[l], 0) for l in range(layer)) + k + 1
        if isinstance(b, Seq):
            return b.reg * per + (const + b.off * per) if per else const
        return const + b * per


class Seq:

    def __init__(self, reg, off):
        self.reg, self.off = reg, off

    @property
    def index(self):
        return self.reg + self.off if self.off else self.reg


def at(b):
    return b.index if isinstance(b, Seq) else b


def need(eng, event, layer, b, k=None):
    v = event.value(layer, b, k)
    if isinstance(v, int) and v <= 1:
        return
    eng.wait_ge(event.sem, v)


def build(nc, d, out):
    ctx = ExitStack()
    with ctx:
        def sb(name, shape, dt=F32):
            return ctx.enter_context(nc.sbuf_tensor(name, shape, dt))

        def sem(name):
            return ctx.enter_context(nc.semaphore(name))

        primed = []

        def event(name, per):
            primed.append(sem(name))
            return Event(primed[-1], per)

        X = sb("X", [P, NB, TT, D])
        Hs = sb("Hs", [P, NB, TT, D])
        w_qkv = {k: sb(f"w_qkv_{k}", [P, 3 * D]) for k in ("rope", "ffn", "cov")}
        w_o = {k: sb(f"w_o_{k}", [P, D]) for k in ("rope", "ffn", "cov")}
        b_qkv = {k: sb(f"b_qkv_{k}", [P, 3, D]) for k in ("rope", "ffn")}
        b_o = {k: sb(f"b_o_{k}", [P, D]) for k in ("rope", "ffn")}
        lncols = sb("lncols", [P, 4])
        w_gate = sb("w_gate", [P, E])
        w_gate_n = sb("w_gate_n", [P, E])
        gate_bias = sb("gate_bias", [P, E])
        lnb = sb("lnb", [P, 2, P])
        w1h = sb("w1h", [P, E, FF], F32R)
        w1l = sb("w1l", [P, E, FF], F32R)
        w1tmp = sb("w1tmp", [P, FF])
        b1c = sb("b1c", [P, E * FC])
        w2 = sb("w2", [P, E * FC, D])
        b2 = sb("b2", [E, D])
        ident = sb("ident", [P, P])
        iota = sb("iota", [P, E])
        ropeA = sb("ropeA", [P, 3, TT, H, HD])
        ropeB = sb("ropeB", [P, 3, TT, H, HD])
        halves = sb("halves", [P, 2 * TT])
        ones = sb("ones", [P, P])

        stats = sb("stats", [P, TT, 6])
        meanvar = sb("meanvar", [P, TT, 2])
        vareps = sb("vareps", [P, TT])
        rstd = sb("rstd", [P, TT])
        stats2 = sb("stats2", [P, TT, 6])
        meanvar2 = sb("meanvar2", [P, TT, 2])
        vareps2 = sb("vareps2", [P, TT])
        rstd2 = sb("rstd2", [P, TT])
        stats3 = sb("stats3", [P, TT, 6])
        meanvar3 = sb("meanvar3", [P, TT, 2])
        vareps3 = sb("vareps3", [P, TT])
        rstd3 = sb("rstd3", [P, TT])
        Y = sb("Y", [P, TT, D])
        Z = sb("Z", [P, TT, D])
        ZT = sb("ZT", [P, T])
        QKV = sb("QKV", [P, 3, TT, D])
        R1 = sb("R1", [P, 3, TT, H, HD])
        R2 = sb("R2", [P, 3, TT, H, HD])
        R = sb("R", [P, 3, TT, D])
        hsum = sb("hsum", [P, 2 * TT * H])
        hmean = sb("hmean", [P, 2 * TT * H])
        hsq = sb("hsq", [P, 2 * TT * H])
        Qst = sb("Qst", [P, TT, H, SL], F32R)
        Kst = sb("Kst", [P, TT, H, SL], F32R)
        QT = sb("QT", [P, NG, T], F32R)
        KT = sb("KT", [P, NG, T], F32R)
        M = sb("M", [P, H, TT])
        Vx = sb("Vx", [P, TT, H, SL])
        Pr = sb("Pr", [P, 2, HG, TT, T])
        OT = sb("OT", [P, NG, T])
        rden = sb("rden", [P, TT, H])
        On = sb("On", [P, TT, D])
        O1 = sb("O1", [P, TT, H, HD])
        O2 = sb("O2", [P, TT, H, HD])
        Or = sb("Or", [P, TT, D])
        OnT = sb("OnT", [P, T])
        U = sb("U", [P, TT, D])
        UT = sb("UT", [P, T])
        TH = sb("TH", [P, NB, T], F32R)
        TL = sb("TL", [P, NB, T], F32R)
        G = sb("G", [P, 2, FC, BLK])
        w1raw = G[:].rearrange("p a c n -> p (a c n)").rearrange("p (e f) -> p e f", e=E)
        LG = sb("LG", [P, NB, TT * E])
        lg = LG[:].rearrange("p b (t e) -> p (b t) e", e=E)
        pe_ = sb("pe_", [P, NT, E])
        col = sb("col", [P, NT])
        col2 = sb("col2", [P, NT])
        top = sb("top", [P, NT, E])
        idx = sb("idx", [P, NT, E], U32)
        pick = sb("pick", [P, NT, E])
        WE = sb("WE", [P, NT, E])
        WT = sb("WT", [E, NT, P])

        bankE = ctx.enter_context(nc.psum_tensor("bankE", [P, HG, TT, T], F32))
        bankO = ctx.enter_context(nc.psum_tensor("bankO", [P, 512], F32))
        bankA = ctx.enter_context(nc.psum_tensor("bankA", [P, 512], F32))
        bankB = ctx.enter_context(nc.psum_tensor("bankB", [P, 512], F32))
        bankC = ctx.enter_context(nc.psum_tensor("bankC", [P, 512], F32))
        front_bank = [bankB, bankA]

        in_x = sem("in_x")
        in_rope = sem("in_rope")
        in_cov = sem("in_cov")
        in_ffn = sem("in_ffn")
        in_moe = sem("in_moe")
        out_done = sem("out_done")
        primed_all = sem("primed_all")
        ffn_only = {"ffn": 1}
        norm_stats = event("norm_stats", 4)
        norm_rstd = event("norm_rstd", 2)
        normed = event("normed", 2)
        norm2_stats = event("norm2_stats", {"ffn": 4})
        norm2_rstd = event("norm2_rstd", {"ffn": 2})
        normed2 = event("normed2", {"ffn": 2})
        res_base = event("res_base", {"rope": 1, "ffn": 1})
        zT = event("zT", 1)
        zT_copied = event("zT_copied", 1)
        proj = event("proj", 2)
        proj_copied = event("proj_copied", 2)
        roped = event("roped", {"rope": 3})
        centred = event("centred", {"cov": 5})
        stacked = event("stacked", {"rope": 4, "ffn": 4, "cov": 8})
        shift_cleared = event("shift_cleared", 1)
        consts_set = sem("consts_set")
        stackT = event("stackT", 4)
        stackT_copied = event("stackT_copied", 4)
        raw_scores = event("raw_scores", H)
        maxed = event("maxed", H)
        shifted = event("shifted", 1)
        shiftT = event("shiftT", 2)
        shiftT_copied = event("shiftT_copied", 2)
        scores = event("scores", 2 * NG)
        exped = event("exped", 2 * NG)
        pv = event("pv", NG)
        pv_copied = event("pv_copied", NG)
        v_ready = event("v_ready", 1)
        outT = event("outT", 2)
        divided = event("divided", 4)
        unroped = event("unroped", {"rope": 3})
        onT = event("onT", 1)
        onT_copied = event("onT_copied", 1)
        wo = event("wo", 1)
        res = event("res", 1)
        w1_split = event("w1_split", {"rope": 3})
        xh = event("xh", ffn_only)
        norm3_stats = event("norm3_stats", {"ffn": 4})
        norm3_rstd = event("norm3_rstd", {"ffn": 2})
        normed3 = event("normed3", {"ffn": 2})
        uT = event("uT", ffn_only)
        uT_copied = event("uT_copied", ffn_only)
        uT_split = event("uT_split", {"ffn": 2})
        gate = event("gate", ffn_only)
        gate_copied = event("gate_copied", ffn_only)
        waits_met = sem("waits_met")
        vx_set = sem("vx_set")
        setup_dve = sem("setup_dve")
        setup_pe = sem("setup_pe")
        gated = sem("gated")
        gate_exp = sem("gate_exp")
        hid = sem("hid")
        hid_act = sem("hid_act")
        expert = sem("expert")
        mixed = sem("mixed")
        weT = sem("weT")
        weT_copied = sem("weT_copied")
        b2mix = sem("b2mix")
        b2_added = sem("b2_added")
        primed += [hid_act, expert, mixed]
        NGATE = 14 + 2 * NT

        def as32(ap):
            return ap.bitcast(F32)

        def banks(b):
            return front_bank[b % 2]

        def apart(eng):
            eng.sem_inc(waits_met, 1)

        block = ctx.enter_context(nc.Block())

        def parts(eng, layer, step):
            step(layer, None, 0)
            with eng.Fori(0, NB - 1) as i:
                step(layer, Seq(i, 0), Seq(i, 1))
            step(layer, NB - 1, None)

        @block.sync
        def _(sp):
            xin = d["x"].rearrange("b (t p) d -> p b t d", p=P)
            for b in range(NB):
                sp.dma_start(X[:, b], xin[:, b]).then_inc(in_x, 16)
            for s in primed:
                sp.sem_inc(s, 1)
            sp.sem_inc(primed_all, 1)
            sp.dma_start(w_gate[:], d["w_gate"]).then_inc(in_ffn, 16)
            sp.dma_start(w_qkv["ffn"][:], d["w_qkv_ffn"]).then_inc(in_ffn, 16)
            sp.dma_start(w_o["ffn"][:], d["w_o_ffn"]).then_inc(in_ffn, 16)
            sp.dma_start(b_qkv["ffn"][:], d["b_qkv_ffn"]).then_inc(in_ffn, 16)
            sp.dma_start(b_o["ffn"][:], d["b_o_ffn"]).then_inc(in_ffn, 16)
            sp.dma_start(lncols[:], d["lncols"]).then_inc(in_ffn, 16)
            sp.dma_start(b1c[:], d["b1c"]).then_inc(in_ffn, 16)
            sp.dma_start(w1raw, d["w1"].rearrange("e p f -> p e f")).then_inc(in_ffn, 16)
            sp.dma_start(w_qkv["cov"][:], d["w_qkv_cov"]).then_inc(in_cov, 16)
            sp.dma_start(w_o["cov"][:], d["w_o_cov"]).then_inc(in_cov, 16)
            sp.dma_start(w2[:], d["w2"].rearrange("e (c p) d -> p (e c) d", p=P)).then_inc(in_moe, 16)
            sp.dma_start(b2[:], d["b2"]).then_inc(in_moe, 16)
            sp.dma_start(iota[:], d["iota"]).then_inc(in_moe, 16)
            sp.wait_ge(b2_added, 8)
            sp.dma_start(out.rearrange("b (t p) d -> p b t d", p=P), X[:]).then_inc(out_done, 16)
            sp.wait_ge(out_done, 16)

        @block.tensor
        def _(pe):
            pe.wait_ge(primed_all, 1)
            mm = nc.tensor.matmul

            def do_scores(layer, b, g):
                need(pe, shiftT_copied, layer, b)
                for pair in range(2):
                    need(pe, exped, layer, b, 2 * g + pair - 1)
                    for j in (2 * pair, 2 * pair + 1):
                        rows = slice(SL * j, SL * j + SL)
                        for kc in range(TT):
                            m = mm(bankE[:, j, kc], KT[rows, g, kc * P:kc * P + P], QT[rows, g, :],
                                   start=True, stop=True)
                    m.then_inc(scores.sem, 1)

            def do_pv(layer, b, g, kc):
                if kc == 0:
                    need(pe, exped, layer, b, 2 * g + 2)
                    need(pe, pv_copied, layer, b, g)
                    if g == 0:
                        need(pe, v_ready, layer, b)
                for j in range(HG):
                    rows = slice(SL * j, SL * j + SL)
                    m = mm(bankO[rows, 0:T], Vx[:, kc, HG * g + j, :], Pr[:, g % 2, j, kc, :],
                           start=(kc == 0), stop=(kc == TT - 1))
                if kc == TT - 1:
                    m.then_inc(pv.sem, 1)

            def do_zT(layer, b):
                need(pe, normed2 if LAYERS[layer] == "ffn" else normed, layer, b)
                need(pe, shiftT_copied, layer, b, 0)
                for t in range(TT):
                    m = nc.tensor.transpose(bankA[:, t * P:t * P + P], Z[:, t, :], ident[:])
                m.then_inc(zT.sem, 1)

            def do_proj(layer, b):
                need(pe, zT_copied, layer, b)
                for t in range(TT):
                    mm(banks(t)[:, 0:3 * D], ZT[:, t * P:t * P + P], w_qkv[LAYERS[layer]][:],
                       start=True, stop=True).then_inc(proj.sem, 1)

            def do_stackT(layer, b):
                need(pe, stacked, layer, b)
                need(pe, shift_cleared, layer, b)
                if not isinstance(b, Seq):
                    pe.wait_ge(consts_set, 2 + 3 * (layer + 1))
                for u, src in enumerate((Kst, Kst, Qst, Qst)):
                    if u < 2:
                        need(pe, proj_copied, layer, b, u + 1)
                    else:
                        need(pe, stackT_copied, layer, b, u - 1)
                    for g in range(NG):
                        m = nc.tensor.transpose(banks(u)[:, g * P:g * P + P],
                                                as32(src[:, u % 2, HG * g:HG * g + HG, :]), ident[:])
                    m.then_inc(stackT.sem, 1)

            def do_raw(layer, b, heads):
                for h in heads:
                    if h < 2:
                        need(pe, stackT_copied, layer, b)
                    else:
                        need(pe, maxed, layer, b, h - 1)
                    g, j = h // HG, h % HG
                    rows = slice(SL * j, SL * j + SL)
                    for t in range(TT):
                        m = mm(banks(h)[:, t * T:t * T + T], QT[rows, g, t * P:t * P + P], KT[rows, g, :],
                               start=True, stop=True)
                    m.then_inc(raw_scores.sem, 1)

            def do_shiftT(layer, b):
                need(pe, maxed, layer, b)
                need(pe, shifted, layer, b)
                for t in range(TT):
                    for g in range(NG):
                        m = nc.tensor.transpose(banks(t)[:, g * P:g * P + P],
                                                as32(Qst[:, t, HG * g:HG * g + HG, :]), ident[:])
                    m.then_inc(shiftT.sem, 1)

            def do_outT(layer, b, t):
                if t == 0:
                    need(pe, pv_copied, layer, b)
                    if layer == 0:
                        need(pe, res, layer, b, 0)
                    elif LAYERS[layer] == "ffn":
                        need(pe, res, layer, b, 0)
                        need(pe, gate_copied, layer, b, 0)
                    else:
                        need(pe, res, layer, b, 0)
                else:
                    need(pe, divided, layer, b, 2 * t)
                for g in range(NG):
                    m = nc.tensor.transpose(bankC[:, g * P:g * P + P], OT[:, g, t * P:t * P + P], ident[:])
                m.then_inc(outT.sem, 1)

            def do_wo(layer, b):
                kind = LAYERS[layer]
                need(pe, divided, layer, b)
                if kind == "rope":
                    need(pe, unroped, layer, b)
                src = Or if kind == "rope" else On
                for t in range(TT):
                    m = nc.tensor.transpose(bankC[:, t * P:t * P + P], src[:, t, :], ident[:])
                m.then_inc(onT.sem, 1)
                need(pe, onT_copied, layer, b)
                for t in range(TT):
                    m = mm(bankC[:, t * D:t * D + D], OnT[:, t * P:t * P + P], w_o[kind][:], start=True, stop=True)
                m.then_inc(wo.sem, 1)
                if kind == "ffn":
                    need(pe, res, layer, b)
                    need(pe, normed3, layer, b)
                    for t in range(TT):
                        m = nc.tensor.transpose(bankC[:, t * P:t * P + P], U[:, t, :], ident[:])
                    m.then_inc(uT.sem, 1)
                    need(pe, uT_copied, layer, b)
                    for t in range(TT):
                        m = mm(bankC[:, t * E:t * E + E], UT[:, t * P:t * P + P], w_gate_n[:], start=True, stop=True)
                    m.then_inc(gate.sem, 1)

            def step(layer, a, f):
                if a is not None:
                    do_scores(layer, a, 1)
                if f is not None:
                    do_zT(layer, f)
                if a is not None:
                    do_pv(layer, a, 0, 0)
                    do_pv(layer, a, 0, 1)
                if f is not None:
                    do_proj(layer, f)
                if a is not None:
                    do_scores(layer, a, 2)
                    do_pv(layer, a, 1, 0)
                    do_pv(layer, a, 1, 1)
                    do_scores(layer, a, 3)
                if f is not None:
                    do_stackT(layer, f)
                heads = [range(0, 4), range(4, 7), range(7, 10), range(10, 13)]
                for n, (g, kc) in enumerate(((2, 0), (2, 1), (3, 0), (3, 1))):
                    if a is not None:
                        do_pv(layer, a, g, kc)
                    if f is not None:
                        do_raw(layer, f, heads[n])
                if a is not None:
                    do_outT(layer, a, 0)
                if f is not None:
                    do_raw(layer, f, range(13, H))
                if a is not None:
                    do_outT(layer, a, 1)
                if f is not None:
                    do_shiftT(layer, f)
                    do_scores(layer, f, 0)
                if a is not None:
                    do_wo(layer, a)

            def setup_ffn():
                pe.wait_ge(in_ffn, 8 * 16)
                pe.wait_ge(setup_dve, 2)
                need(pe, res, 0, NB - 1)
                need(pe, pv_copied, 0, NB - 1)
                mm(bankC[:, 0:3 * D], lnb[:, 0, :], w_qkv["ffn"][:], start=True, stop=True).then_inc(setup_pe, 1)
                for n in range(E * FC):
                    mm(bankO[:, n:n + 1], w1raw[:, n // FC, (n % FC) * P:(n % FC) * P + P], lncols[:, 3:4],
                       start=True, stop=True)
                mm(bankO[:, 64:64 + E], lnb[:, 1, :], w_gate[:], start=True, stop=True).then_inc(setup_pe, 1)
                pe.wait_ge(setup_dve, 7)

            def mixture(layer, ph):
                need(pe, uT_split, layer, NB - 1)
                need(pe, exped, layer, NB - 1)
                if ph == 0:
                    pe.wait_ge(in_moe, 3 * 16)
                need(pe, w1_split, layer, 0, 0)

                def hidden(j, e):
                    for c in range(FC):
                        base = ph * NBLK * E * FC + e * FC + c - FC + 1
                        v = j * (E * FC) + (base + 1)
                        if e or ph:
                            pe.wait_ge(hid_act, v)
                        else:
                            pe.wait_ge(hid_act, j * (E * FC) + 1)
                        w = slice(c * P, c * P + P)
                        n = (e * FC + c) % 4
                        acc = bankE[:, n].rearrange("p k q -> p (k q)")
                        th = TH[:].rearrange("p b t -> p (b t)").rearrange("p (j n) -> p j n", j=NBLK)[:, j]
                        tl = TL[:].rearrange("p b t -> p (b t)").rearrange("p (j n) -> p j n", j=NBLK)[:, j]
                        mm(acc, w1h[:, e, w], th, start=True, stop=False)
                        mm(acc, w1h[:, e, w], tl, start=False, stop=False)
                        mm(acc, w1l[:, e, w], th, start=False, stop=True).then_inc(hid, 1)

                def outputs(j, e):
                    pe.wait_ge(hid_act, j * (E * FC) + (ph * NBLK * E * FC + (e + 1) * FC + 1))
                    if e >= 2 or ph:
                        pe.wait_ge(mixed, j * (E * BT) + (ph * NBLK * E * BT + (e - 1) * BT + 1))
                    else:
                        pe.wait_ge(mixed, j * (E * BT) + 1)
                    for t in range(BT):
                        for c in range(FC):
                            m = mm(banks(e)[:, t * D:t * D + D], G[:, e % 2, c, t * P:t * P + P],
                                   w2[:, e * FC + c, :], start=(c == 0), stop=(c == FC - 1))
                    m.then_inc(expert, 1)

                with pe.Fori(0, NBLK) as j:
                    hidden(j, 0)
                    for e in range(E):
                        if e + 1 < E:
                            hidden(j, e + 1)
                        outputs(j, e)

                pe.wait_ge(gated, (ph + 1) * NGATE)
                need(pe, gate_copied, layer, NB - 1)
                need(pe, pv_copied, layer, NB - 1)
                wb = [bankC, bankO]
                for q in range(4):
                    if q >= 2:
                        pe.wait_ge(weT_copied, 4 * ph + q - 1)
                    for t in range(4):
                        m = nc.tensor.transpose(wb[q % 2][0:E, t * P:t * P + P], WE[:, 4 * q + t, :], ident[:])
                    m.then_inc(weT, 1)
                for q in range(4):
                    if q < 2:
                        pe.wait_ge(weT_copied, 4 * ph + 3 + q)
                    else:
                        pe.wait_ge(b2_added, 4 * ph + q - 1)
                    for t in range(4):
                        m = mm(wb[q % 2][:, t * D:t * D + D], WT[:, 4 * q + t, :], b2[:], start=True, stop=True)
                    m.then_inc(b2mix, 1)

            for layer in range(len(LAYERS)):
                if layer == 0:
                    pe.wait_ge(in_rope, 6 * 16)
                if layer == 1:
                    setup_ffn()
                if layer == 2:
                    pe.wait_ge(in_cov, 2 * 16)
                if layer >= 2:
                    ph = layer - 2
                    if layer == 2:
                        pe.wait_ge(mixed, NBLK * E * BT + 1)
                        pe.wait_ge(b2_added, 4)
                        pe.wait_ge(hid_act, NBLK * E * FC + 1)
                parts(pe, layer, step)
                if LAYERS[layer] == "ffn":
                    mixture(layer, layer // 2)

        @block.scalar
        def _(act):
            act.dma_start(w_qkv["rope"][:], d["w_qkv_rope"]).then_inc(in_rope, 16)
            act.dma_start(ident[:], d["ident"]).then_inc(in_rope, 16)
            act.dma_start(b_qkv["rope"][:], d["b_qkv_rope"]).then_inc(in_rope, 16)
            act.dma_start(ropeA[:], d["ropeA"]).then_inc(in_rope, 16)
            act.dma_start(ropeB[:], d["ropeB"]).then_inc(in_rope, 16)
            act.dma_start(w_o["rope"][:], d["w_o_rope"]).then_inc(in_rope, 16)
            act.dma_start(b_o["rope"][:], d["b_o_rope"]).then_inc(in_rope, 16)
            act.wait_ge(primed_all, 1)

            def copy(dst, src):
                return nc.scalar.activation(dst, src, ACT.Copy)

            def do_exp(layer, b, g):
                for pair in range(2):
                    need(act, scores, layer, b, 2 * g + pair + 1)
                    need(act, pv, layer, b, g - 1)
                    js = slice(2 * pair, 2 * pair + 2)
                    nc.scalar.activation(Pr[:, g % 2, js], bankE[:, js], ACT.Exp,
                                         scale=EXP_SCALE[LAYERS[layer]]).then_inc(exped.sem, 1)

            def do_zT(layer, b):
                need(act, zT, layer, b)
                need(act, proj, layer, b, 0)
                copy(ZT[:], bankA[:, 0:T]).then_inc(zT_copied.sem, 1)

            def do_pv(layer, b, g):
                need(act, pv, layer, b, g + 1)
                if g == 0:
                    need(act, outT, layer, b, 0)
                copy(OT[:, g, :], bankO[:, 0:T]).then_inc(pv_copied.sem, 1)

            def do_stackT(layer, b):
                for u, dst in enumerate((KT, KT, QT, QT)):
                    need(act, stackT, layer, b, u + 1)
                    if u == 0:
                        need(act, scores, layer, b, 0)
                    copy(dst[:, :, (u % 2) * P:(u % 2) * P + P],
                         banks(u)[:].rearrange("p (g t) -> p g t", g=NG)).then_inc(stackT_copied.sem, 1)

            def do_shiftT(layer, b):
                for t in range(TT):
                    need(act, shiftT, layer, b, t + 1)
                    if t == 0:
                        need(act, raw_scores, layer, b)
                    copy(QT[:, :, t * P:t * P + P],
                         banks(t)[:].rearrange("p (g t) -> p g t", g=NG)).then_inc(shiftT_copied.sem, 1)

            def tail(layer, b):
                need(act, onT, layer, b)
                need(act, wo, layer, b, 0)
                copy(OnT[:], bankC[:, 0:T]).then_inc(onT_copied.sem, 1)
                if LAYERS[layer] == "ffn":
                    need(act, uT, layer, b)
                    need(act, gate, layer, b, 0)
                    need(act, uT_split, layer, b, 0)
                    copy(UT[:], bankC[:, 0:T]).then_inc(uT_copied.sem, 1)
                    need(act, gate, layer, b)
                    copy(LG[:, at(b), :], bankC[:, 0:TT * E]).then_inc(gate_copied.sem, 1)

            def step(layer, a, f):
                if a is not None:
                    do_exp(layer, a, 1)
                if f is not None:
                    do_zT(layer, f)
                if a is not None:
                    do_pv(layer, a, 0)
                    do_exp(layer, a, 2)
                    do_pv(layer, a, 1)
                    do_exp(layer, a, 3)
                if f is not None:
                    do_stackT(layer, f)
                if a is not None:
                    do_pv(layer, a, 2)
                    do_pv(layer, a, 3)
                if f is not None:
                    do_shiftT(layer, f)
                    do_exp(layer, f, 0)
                if a is not None:
                    tail(layer, a)

            def mixture(layer, ph):
                act.wait_ge(gated, ph * NGATE + 3)
                nc.scalar.activation(pe_[:], lg, ACT.Exp).then_inc(gate_exp, 1)
                need(act, pv, layer, NB - 1)
                with act.Fori(0, NBLK) as j:
                    for e in range(E):
                        if e >= 2 or ph:
                            act.wait_ge(expert, j * E + (ph * NBLK * E + e - 1 + 1))
                        else:
                            act.wait_ge(expert, j * E + 1)
                        for c in range(FC):
                            act.wait_ge(hid, j * (E * FC) + (ph * NBLK * E * FC + e * FC + c + 1))
                            n = (e * FC + c) % 4
                            nc.scalar.activation(G[:, e % 2, c, :], bankE[:, n].rearrange("p k q -> p (k q)"),
                                                 ACT.Gelu_apprx_tanh,
                                                 bias=b1c[:, e * FC + c:e * FC + c + 1]).then_inc(hid_act, 1)
                for q in range(4):
                    act.wait_ge(weT, 4 * ph + q + 1)
                    if q == 0 and ph:
                        act.wait_ge(b2mix, 4 * ph)
                    wb = [bankC, bankO][q % 2]
                    copy(WT[:, 4 * q:4 * q + 4, :], wb[0:E, :].rearrange("e (t p) -> e t p", t=4)).then_inc(weT_copied, 1)

            for layer in range(len(LAYERS)):
                if layer == 1:
                    act.wait_ge(setup_dve, 7)
                parts(act, layer, step)
                if LAYERS[layer] == "ffn":
                    mixture(layer, layer // 2)

        @block.vector
        def _(dve):
            dve.wait_ge(primed_all, 1)
            v = nc.vector
            tt = v.tensor_tensor

            def stats_of(layer, b, ev, src, st, mv):
                apart(dve)
                for t in range(TT):
                    v.bn_stats(st[:, t, :], src[:, t, :]).then_inc(ev.sem, 1)
                for t in range(TT):
                    need(dve, ev, layer, b, t + 1)
                    apart(dve)
                    v.bn_aggr(mv[:, t, :], st[:, t, :]).then_inc(ev.sem, 1)

            def normalise(layer, b, ev, dst, src, mv, rs):
                for t in range(TT):
                    v.tensor_scalar(dst[:, t, :], src[:, t, :], mv[:, t, 0:1], rs[:, t:t + 1],
                                    ALU.subtract, ALU.mult).then_inc(ev.sem, 1)

            def norm(layer, b):
                ffn = LAYERS[layer] == "ffn"
                if layer == 0:
                    dve.wait_ge(in_x, NB * 16)
                elif not ffn:
                    dve.wait_ge(b2_added, 4 * (layer // 2))
                else:
                    need(dve, res, layer - 1, b)
                x = X[:, at(b)]
                stats_of(layer, b, norm_stats, x, stats, meanvar)
                need(dve, norm_rstd, layer, b)
                first = Y if ffn else Z
                if ffn:
                    need(dve, res_base, layer, b, 0)
                else:
                    need(dve, zT, layer, b, 0)
                normalise(layer, b, normed, first, x, meanvar, rstd)
                if ffn:
                    need(dve, normed, layer, b)
                    stats_of(layer, b, norm2_stats, Y, stats2, meanvar2)
                    need(dve, norm2_rstd, layer, b)
                    need(dve, zT, layer, b, 0)
                    normalise(layer, b, normed2, Z, Y, meanvar2, rstd2)

            def do_proj(layer, b):
                kind = LAYERS[layer]
                need(dve, v_ready, layer, b, 0)
                for t in range(TT):
                    need(dve, proj, layer, b, t + 1)
                    src = banks(t)[:, 0:3 * D].rearrange("p (c d) -> p c d", c=3)
                    if kind == "cov":
                        v.tensor_copy(QKV[:, :, t, :], src).then_inc(proj_copied.sem, 1)
                    else:
                        tt(QKV[:, :, t, :], src, b_qkv[kind][:], ALU.add).then_inc(proj_copied.sem, 1)

            def heads(ap):
                return ap.rearrange("p c t (h x) -> p (c t h) x", x=HD)

            def rope_operands(ap):
                half = ap.rearrange("p n (w o) -> p n w o", o=2)
                n = ap.shape[1]
                ev = half[:, :, :, 0].unsqueeze(2).broadcast_to([P, n, 2, HD // 2])
                od = half[:, :, :, 1].unsqueeze(2).broadcast_to([P, n, 2, HD // 2])
                return ev, od

            def flat(ap):
                return ap.rearrange("p c t h (u w) -> p (c t h) u w", u=2)

            def rope(layer, b):
                need(dve, proj_copied, layer, b)
                ev, od = rope_operands(heads(QKV[:]))
                tt(flat(R1[:]), ev, flat(ropeA[:]), ALU.mult).then_inc(roped.sem, 1)
                tt(flat(R2[:]), od, flat(ropeB[:]), ALU.mult).then_inc(roped.sem, 1)
                need(dve, roped, layer, b, 2)
                tt(heads(R[:]), R1[:].rearrange("p c t h x -> p (c t h) x"),
                   R2[:].rearrange("p c t h x -> p (c t h) x"), ALU.add).then_inc(roped.sem, 1)

            def centre(layer, b):
                need(dve, proj_copied, layer, b)
                n = 2 * TT * H
                qk = heads(QKV[:, 0:2])
                dst = heads(R[:, 0:2])
                v.tensor_reduce(hsum[:], qk, AX.X, ALU.add).then_inc(centred.sem, 1)
                need(dve, centred, layer, b, 1)
                v.tensor_scalar(hmean[:], hsum[:], 1.0 / HD, None, ALU.mult).then_inc(centred.sem, 1)
                need(dve, centred, layer, b, 2)
                tt(dst, qk, hmean[:].unsqueeze(2).broadcast_to([P, n, HD]), ALU.subtract).then_inc(centred.sem, 1)
                need(dve, centred, layer, b, 3)
                sq = R1[:, 0:2].rearrange("p c t h x -> p (c t h) x")
                tt(sq, dst, dst, ALU.mult).then_inc(centred.sem, 1)
                need(dve, centred, layer, b, 4)
                v.tensor_reduce(hsq[:], sq, AX.X, ALU.add).then_inc(centred.sem, 1)

            def stack(layer, b):
                kind = LAYERS[layer]
                if kind == "ffn":
                    need(dve, proj_copied, layer, b)
                elif kind == "rope":
                    need(dve, roped, layer, b)
                else:
                    need(dve, centred, layer, b)
                    dve.wait_ge(consts_set, 2 + 3 * (layer + 1))
                need(dve, shiftT, layer, b, 0)
                src = QKV if kind == "ffn" else R
                n = TT * H
                q = src[:, 0].rearrange("p t (h x) -> p (t h) x", x=HD)
                k = src[:, 1].rearrange("p t (h x) -> p (t h) x", x=HD)
                qs = Qst[:].rearrange("p t h s -> p (t h) s")
                ks = Kst[:].rearrange("p t h s -> p (t h) s")
                rep = lambda ap: ap.unsqueeze(2).broadcast_to([P, n, 2, HD])
                v.tensor_copy(qs[:, :, 0:2 * HD].rearrange("p n (r x) -> p n r x", r=2), rep(q)).then_inc(stacked.sem, 1)
                k_hi = ks[:, :, 0:4 * HD].rearrange("p n (r y) -> p n r y", r=2)[:, :, :, 0:HD]
                v.tensor_copy(k_hi, rep(k)).then_inc(stacked.sem, 1)
                if kind == "cov":
                    hq = hsq[:, 0:n].unsqueeze(2)
                    hk = hsq[:, n:2 * n].unsqueeze(2)
                    inv = 1.0 / (HD - 1)
                    v.tensor_scalar(qs[:, :, 24:26], hq.broadcast_to([P, n, 2]), inv, None,
                                    ALU.mult).then_inc(stacked.sem, 1)
                    v.tensor_scalar(ks[:, :, 24:28].rearrange("p n (r y) -> p n r y", y=2)[:, :, :, 0],
                                    hk.broadcast_to([P, n, 2]), inv, None, ALU.mult).then_inc(stacked.sem, 1)
                need(dve, stacked, layer, b, 4 if kind == "cov" else 2)
                tt(qs[:, :, 2 * HD:3 * HD], q, as32(qs[:, :, 0:HD]), ALU.subtract).then_inc(stacked.sem, 1)
                tt(ks[:, :, HD:2 * HD], k, as32(ks[:, :, 0:HD]), ALU.subtract).then_inc(stacked.sem, 1)
                if kind == "cov":
                    v.scalar_tensor_tensor(qs[:, :, 26:27], hq, inv, as32(qs[:, :, 24:25]),
                                           ALU.mult, ALU.subtract).then_inc(stacked.sem, 1)
                    v.scalar_tensor_tensor(ks[:, :, 25:26], hk, inv, as32(ks[:, :, 24:25]),
                                           ALU.mult, ALU.subtract).then_inc(stacked.sem, 1)

            def do_max(layer, b, hs):
                for h in hs:
                    need(dve, raw_scores, layer, b, h + 1)
                    v.tensor_reduce(M[:, h, :], banks(h)[:].rearrange("p (t k) -> p t k", t=TT),
                                    AX.X, ALU.max).then_inc(maxed.sem, 1)

            def shift(layer, b):
                need(dve, maxed, layer, b)
                need(dve, stackT, layer, b)
                v.tensor_scalar(Qst[:, :, :, SHIFT], M[:].rearrange("p h t -> p t h"), -1.0, None,
                                ALU.mult).then_inc(shifted.sem, 1)

            def divide(layer, b, t):
                need(dve, outT, layer, b, t + 1)
                if t == 0:
                    need(dve, onT, layer, b, 0)
                o = bankC[:].rearrange("p (h s) -> p h s", s=SL)
                v.reciprocal(rden[:, t, :], o[:, :, HD]).then_inc(divided.sem, 1)
                need(dve, divided, layer, b, 2 * t + 1)
                tt(On[:, t, :].rearrange("p (h x) -> p h x", x=HD), o[:, :, 0:HD],
                   rden[:, t, :].unsqueeze(2).broadcast_to([P, H, HD]), ALU.mult).then_inc(divided.sem, 1)

            def unrope(layer, b):
                need(dve, divided, layer, b)
                ev, od = rope_operands(On[:].rearrange("p t (h x) -> p (t h) x", x=HD))
                f = lambda ap: ap.rearrange("p t h (u w) -> p (t h) u w", u=2)
                tt(f(O1[:]), ev, f(ropeA[:, 0]), ALU.mult).then_inc(unroped.sem, 1)
                tt(f(O2[:]), od, f(ropeB[:, 0]), ALU.mult).then_inc(unroped.sem, 1)
                need(dve, unroped, layer, b, 2)
                need(dve, onT, layer, b, 0)
                v.scalar_tensor_tensor(Or[:].rearrange("p t d -> p (t d)"), O1[:].rearrange("p t h x -> p (t h x)"),
                                       -1.0, O2[:].rearrange("p t h x -> p (t h x)"),
                                       ALU.mult, ALU.subtract).then_inc(unroped.sem, 1)

            def tail(layer, b):
                kind = LAYERS[layer]
                if kind == "rope":
                    unrope(layer, b)
                need(dve, wo, layer, b)
                if kind != "cov":
                    need(dve, res_base, layer, b)
                dst = Hs if kind == "ffn" else X
                tt(dst[:, at(b)], bankC[:, 0:T].rearrange("p (t d) -> p t d", t=TT), dst[:, at(b)],
                   ALU.add).then_inc(res.sem, 1)
                if kind == "ffn":
                    need(dve, res, layer, b)
                    stats_of(layer, b, norm3_stats, Hs[:, at(b)], stats3, meanvar3)
                    need(dve, norm3_rstd, layer, b)
                    need(dve, uT, layer, b, 0)
                    normalise(layer, b, normed3, U, Hs[:, at(b)], meanvar3, rstd3)

            def step(layer, a, f):
                if f is not None:
                    norm(layer, f)
                    do_proj(layer, f)
                    if LAYERS[layer] == "rope":
                        rope(layer, f)
                    if LAYERS[layer] == "cov":
                        centre(layer, f)
                    stack(layer, f)
                    do_max(layer, f, range(0, 13))
                if a is not None:
                    divide(layer, a, 0)
                if f is not None:
                    do_max(layer, f, range(13, H))
                    shift(layer, f)
                if a is not None:
                    divide(layer, a, 1)
                    tail(layer, a)

            def setup_ffn():
                dve.wait_ge(in_ffn, 8 * 16)
                v.tensor_scalar(lnb[:, 0, :], ones[:], lncols[:, 1:2], None, ALU.mult).then_inc(setup_dve, 1)
                v.tensor_scalar(lnb[:, 1, :], ones[:], lncols[:, 3:4], None, ALU.mult).then_inc(setup_dve, 1)
                dve.wait_ge(setup_pe, 2)
                tt(b_qkv["ffn"][:], bankC[:, 0:3 * D].rearrange("p (c d) -> p c d", c=3), b_qkv["ffn"][:],
                   ALU.add).then_inc(setup_dve, 1)
                tt(b1c[:], bankO[:, 0:E * FC], b1c[:], ALU.add).then_inc(setup_dve, 1)
                v.tensor_copy(gate_bias[:], bankO[:, 64:64 + E]).then_inc(setup_dve, 1)
                v.tensor_scalar(w_qkv["ffn"][:], w_qkv["ffn"][:], lncols[:, 0:1], None,
                                ALU.mult).then_inc(setup_dve, 1)
                v.tensor_scalar(w_gate_n[:], w_gate[:], lncols[:, 2:3], None, ALU.mult).then_inc(setup_dve, 1)
                dve.wait_ge(setup_dve, 7)

            def mixture(layer, ph):
                done = [ph * NGATE]

                def then(ins):
                    ins.then_inc(gated, 1)
                    done[0] += 1
                    dve.wait_ge(gated, done[0])

                def across(c):
                    return c.unsqueeze(2).broadcast_to([P, NT, E])

                if ph == 0:
                    dve.wait_ge(in_moe, 3 * 16)
                need(dve, gate_copied, layer, NB - 1)
                then(tt(lg, lg, gate_bias[:].unsqueeze(1).broadcast_to([P, NT, E]), ALU.add))
                then(v.tensor_reduce(col[:], lg, AX.X, ALU.max))
                then(tt(lg, lg, across(col[:]), ALU.subtract))
                dve.wait_ge(gate_exp, ph + 1)
                then(v.tensor_reduce(col[:], pe_[:], AX.X, ALU.add))
                then(v.reciprocal(col2[:], col[:]))
                then(tt(pe_[:], pe_[:], across(col2[:]), ALU.mult))
                for t in range(NT):
                    then(v.max(top[:, t, :], pe_[:, t, :]))
                for t in range(NT):
                    then(v.max_index(idx[:, t, :], top[:, t, :], pe_[:, t, :]))
                then(tt(col[:], top[:, :, 0], top[:, :, 1], ALU.add))
                then(v.reciprocal(col2[:], col[:]))
                then(tt(top[:, :, 0:2], top[:, :, 0:2], col2[:].unsqueeze(2).broadcast_to([P, NT, 2]), ALU.mult))
                io = iota[:].unsqueeze(1).broadcast_to([P, NT, E])
                then(tt(pick[:], io, across(idx[:, :, 0]), ALU.is_equal))
                if ph:
                    dve.wait_ge(weT, 4 * ph)
                then(tt(WE[:], pick[:], across(top[:, :, 0]), ALU.mult))
                then(tt(pick[:], io, across(idx[:, :, 1]), ALU.is_equal))
                then(tt(pick[:], pick[:], across(top[:, :, 1]), ALU.mult))
                then(tt(WE[:], WE[:], pick[:], ALU.add))

                need(dve, xh, layer, NB - 1)
                xt = X[:].rearrange("p b t d -> p (b t) d").rearrange("p (j t) d -> p j t d", j=NBLK)
                we = WE[:].rearrange("p (j t) e -> p j t e", j=NBLK)
                with dve.Fori(0, NBLK) as j:
                    for e in range(E):
                        dve.wait_ge(expert, j * E + (ph * NBLK * E + e + 1 + 1))
                        for t in range(BT):
                            if e or ph:
                                dve.wait_ge(mixed, j * (E * BT) + (ph * NBLK * E * BT + (e - 1) * BT + t + 1 + 1))
                            v.scalar_tensor_tensor(xt[:, j, t, :], banks(e)[:, t * D:t * D + D],
                                                   we[:, j, t, e:e + 1], xt[:, j, t, :],
                                                   ALU.mult, ALU.add).then_inc(mixed, 1)
                dve.wait_ge(mixed, (ph + 1) * NBLK * E * BT + 1)
                for q in range(4):
                    dve.wait_ge(b2mix, 4 * ph + q + 1)
                    xq = X[:].rearrange("p b t d -> p (b t) d")[:, 4 * q:4 * q + 4, :]
                    tt(xq, [bankC, bankO][q % 2][:].rearrange("p (t d) -> p t d", t=4), xq,
                       ALU.add).then_inc(b2_added, 1)

            dve.wait_ge(in_rope, 7 * 16)
            dve.wait_ge(consts_set, 2)
            for layer in range(len(LAYERS)):
                if layer == 1:
                    setup_ffn()
                parts(dve, layer, step)
                if LAYERS[layer] == "ffn":
                    mixture(layer, layer // 2)

        @block.gpsimd
        def _(pool):
            pool.wait_ge(primed_all, 1)
            g = nc.gpsimd
            g.memset(ones[:], 1.0).then_inc(consts_set, 1)
            g.memset(halves[:], -0.5).then_inc(consts_set, 1)
            g.memset(Vx[:], 0.0).then_inc(vx_set, 1)
            pool.wait_ge(vx_set, 1)
            g.memset(Vx[:, :, :, HD:HD + 1], 1.0).then_inc(vx_set, 1)
            pool.wait_ge(vx_set, 2)

            def power(layer, b, stats_ev, ev, mv, ve, rs, applied):
                need(pool, stats_ev, layer, b)
                need(pool, applied, layer, b, 0)
                apart(pool)
                g.tensor_scalar(ve[:], mv[:, :, 1], EPS, None, ALU.add).then_inc(ev.sem, 1)
                need(pool, ev, layer, b, 1)
                g.tensor_tensor(rs[:], ve[:], halves[:, 0:TT], ALU.pow).then_inc(ev.sem, 1)

            def step(layer, a, f):
                kind = LAYERS[layer]
                if f is not None:
                    power(layer, f, norm_stats, norm_rstd, meanvar, vareps, rstd, normed)
                    if kind == "ffn":
                        power(layer, f, norm2_stats, norm2_rstd, meanvar2, vareps2, rstd2, normed2)
                    need(pool, shiftT, layer, f, 0)
                    apart(pool)
                    if not isinstance(f, Seq):
                        pool.wait_ge(consts_set, 2 + 3 * (layer + 1))
                    g.memset(as32(Qst[:, :, :, SHIFT:SHIFT + 1]), 0.0).then_inc(shift_cleared.sem, 1)
                    if kind != "cov":
                        need(pool, normed, layer, f)
                        src = Y[:] if kind == "ffn" else X[:, at(f)]
                        dst = Hs[:, at(f)] if kind == "ffn" else X[:, at(f)]
                        g.tensor_tensor(dst, src, b_o[kind][:].unsqueeze(1).broadcast_to([P, TT, D]),
                                        ALU.add).then_inc(res_base.sem, 1)
                    need(pool, roped if kind == "rope" else proj_copied, layer, f)
                    need(pool, pv, layer, f, 0)
                    apart(pool)
                    src = R if kind == "rope" else QKV
                    g.tensor_copy(Vx[:, :, :, 0:HD].rearrange("p t h x -> p (t h) x"),
                                  src[:, 2].rearrange("p t (h x) -> p (t h) x", x=HD)).then_inc(v_ready.sem, 1)
                if a is not None:
                    if kind == "rope":
                        e = at(a)
                        if not isinstance(a, Seq):
                            e = NB - 1
                        pool.wait_ge(in_ffn, 8 * 16)
                        need(pool, w1_split, layer, a, 0)
                        g.tensor_tensor(w1tmp[:], w1raw[:, e, :], lncols[:, 2:3].broadcast_to([P, FF]), ALU.mult).then_inc(w1_split.sem, 1)
                        need(pool, w1_split, layer, a, 1)
                        apart(pool)
                        g.tensor_copy(w1h[:, e, :], w1tmp[:]).then_inc(w1_split.sem, 1)
                        need(pool, w1_split, layer, a, 2)
                        g.tensor_tensor(w1l[:, e, :], w1tmp[:], as32(w1h[:, e, :]), ALU.subtract).then_inc(w1_split.sem, 1)
                    if kind == "ffn":
                        need(pool, res, layer, a)
                        g.tensor_tensor(X[:, at(a)], X[:, at(a)], Hs[:, at(a)], ALU.add).then_inc(xh.sem, 1)
                        power(layer, a, norm3_stats, norm3_rstd, meanvar3, vareps3, rstd3, normed3)
                        need(pool, uT_copied, layer, a)
                        apart(pool)
                        g.tensor_copy(TH[:, at(a), :], UT[:]).then_inc(uT_split.sem, 1)
                        need(pool, uT_split, layer, a, 1)
                        g.tensor_tensor(TL[:, at(a), :], UT[:], as32(TH[:, at(a), :]), ALU.subtract).then_inc(uT_split.sem, 1)

            for layer in range(len(LAYERS)):
                if layer:
                    need(pool, shiftT, layer - 1, NB - 1)
                base = 2 + 3 * layer
                if layer == 1:
                    pool.wait_ge(in_ffn, 8 * 16)
                if layer == 0:
                    pool.wait_ge(in_rope, 7 * 16)
                g.memset(as32(Qst[:, :, :, 3 * HD:SL]), 0.0).then_inc(consts_set, 1)
                g.memset(as32(Kst[:, :, :, 3 * HD:SL]), 0.0).then_inc(consts_set, 1)
                pool.wait_ge(consts_set, base + 2)
                g.memset(as32(Kst[:, :, :, SHIFT:SHIFT + 1]), 1.0).then_inc(consts_set, 1)
                parts(pool, layer, step)


_OUT = (NB, T, D)


def kernel(**inputs):
    import numpy as np
    import concourse.bacc as bacc
    from concourse.bass_utils import run_bass_kernel_spmd

    i = {k: np.asarray(v) for k, v in inputs.items()}

    def rows(a):
        return np.ascontiguousarray(np.tile(a.reshape(1, -1), (P, 1)))

    theta = (10000.0 ** (-np.arange(0, HD, 2, dtype=np.float32)[None, :] / HD)).astype(np.float32)
    freqs = np.arange(T, dtype=np.float32)[:, None] * theta
    table = np.concatenate([np.cos(freqs), np.sin(freqs)], axis=-1).astype(np.float32)
    cos, sin = table[:, ::2], table[:, 1::2]

    def spread(a):
        a = a.reshape(TT, P, HD).transpose(1, 0, 2)[:, None, :, None, :]
        return np.ascontiguousarray(np.broadcast_to(a, (P, 3, TT, H, HD)))

    a = {
        "x": i["L0_attn_a_x"],
        "w_qkv_rope": np.concatenate([i["L0_attn_a_Wq"].T, i["L0_attn_a_Wk"].T, i["L0_attn_a_Wv"].T], axis=1),
        "w_o_rope": i["L0_attn_a_Wo"].T,
        "b_qkv_rope": rows(np.concatenate([i["L0_attn_a_bq"], i["L0_attn_a_bk"], i["L0_attn_a_bv"]])),
        "b_o_rope": rows(i["L0_attn_a_bo"]),
        "w_qkv_cov": np.concatenate([i["L0_attn_b_Wq"].T, i["L0_attn_b_Wk"].T, i["L0_attn_b_Wv"].T], axis=1),
        "w_o_cov": i["L0_attn_b_Wo"].T,
        "w_qkv_ffn": i["L0_ffn_w_qkv"],
        "w_o_ffn": i["L0_ffn_w_o"],
        "b_qkv_ffn": rows(i["L0_ffn_b_qkv"]),
        "b_o_ffn": rows(i["L0_ffn_b_o"]),
        "lncols": np.stack([i["L0_ffn_ln1_w"], i["L0_ffn_ln1_b"], i["L0_ffn_ln2_w"], i["L0_ffn_ln2_b"]], axis=1),
        "w_gate": i["L0_ffn_w_gate"],
        "w1": i["L0_ffn_w1"],
        "b1c": i["L0_ffn_b1"].reshape(E * FC, P).T,
        "w2": i["L0_ffn_w2"],
        "b2": i["L0_ffn_b2"],
        "ident": np.eye(P, dtype=np.float32),
        "iota": rows(np.arange(E, dtype=np.float32)),
        "ropeA": spread(np.concatenate([cos, sin], axis=-1)),
        "ropeB": spread(np.concatenate([-sin, cos], axis=-1)),
    }
    for k in ("b_qkv_rope", "b_qkv_ffn"):
        a[k] = a[k].reshape(P, 3, D)
    nc = bacc.Bacc("TRN2", target_bir_lowering=False, num_devices=1)
    arrays, args = {}, {}
    for name, x in a.items():
        x = np.ascontiguousarray(x)
        arrays[f"in_{name}"] = x
        args[name] = nc.dram_tensor(f"in_{name}", x.shape, mybir.dt.from_np(x.dtype), kind="ExternalInput").ap()
    out = nc.dram_tensor("out_x", _OUT, F32, kind="ExternalOutput").ap()
    build(nc, args, out)
    r = run_bass_kernel_spmd(nc, [arrays], core_ids=[0])
    return r.results[0]["out_x"]
```

```python
import concourse.bass as bass
from concourse import mybir
from contextlib import ExitStack

F32 = mybir.dt.float32
F32R = mybir.dt.float32r
U32 = mybir.dt.uint32
ALU = mybir.AluOpType
ACT = mybir.ActivationFunctionType
AX = mybir.AxisListType

P = 128
D = 128
NB = 8
T = 256
TT = T // P
NT = NB * TT
H = 16
HD = D // H
SL = 32
HG = P // SL
NG = H // HG
SHIFT = 27
E = 8
FF = 512
FC = FF // P
BLK = 512
NBLK = NB * T // BLK
BT = BLK // P
EPS = 1e-5
SCALE = float(HD) ** -0.5
LAYERS = ["rope", "ffn", "cov", "ffn"]
EXP_SCALE = {"rope": SCALE, "ffn": SCALE, "cov": 1.0 / HD}


class Event:

    def __init__(self, sem, per):
        self.sem = sem
        self.per = per if isinstance(per, dict) else {k: per for k in LAYERS}

    def value(self, layer, b, k):
        per = self.per.get(LAYERS[layer], 0)
        k = per if k is None else k
        const = sum(NB * self.per.get(LAYERS[l], 0) for l in range(layer)) + k + 1
        if isinstance(b, Seq):
            return b.reg * per + (const + b.off * per) if per else const
        return const + b * per


class Seq:

    def __init__(self, reg, off):
        self.reg, self.off = reg, off

    @property
    def index(self):
        return self.reg + self.off if self.off else self.reg


def at(b):
    return b.index if isinstance(b, Seq) else b


def need(eng, event, layer, b, k=None):
    v = event.value(layer, b, k)
    if isinstance(v, int) and v <= 1:
        return
    eng.wait_ge(event.sem, v)


def build(nc, d, out):
    ctx = ExitStack()
    with ctx:
        def sb(name, shape, dt=F32):
            return ctx.enter_context(nc.sbuf_tensor(name, shape, dt))

        def sem(name):
            return ctx.enter_context(nc.semaphore(name))

        primed = []

        def event(name, per):
            primed.append(sem(name))
            return Event(primed[-1], per)

        X = sb("X", [P, NB, TT, D])
        Hs = sb("Hs", [P, NB, TT, D])
        w_qkv = {k: sb(f"w_qkv_{k}", [P, 3 * D]) for k in ("rope", "ffn", "cov")}
        w_o = {k: sb(f"w_o_{k}", [P, D]) for k in ("rope", "ffn", "cov")}
        b_qkv = {k: sb(f"b_qkv_{k}", [P, 3, D]) for k in ("rope", "ffn")}
        b_o = {k: sb(f"b_o_{k}", [P, D]) for k in ("rope", "ffn")}
        lncols = sb("lncols", [P, 4])
        w_gate = sb("w_gate", [P, E])
        w_gate_n = sb("w_gate_n", [P, E])
        gate_bias = sb("gate_bias", [P, E])
        lnb = sb("lnb", [P, 2, P])
        w1h = sb("w1h", [P, E, FF], F32R)
        w1l = sb("w1l", [P, E, FF], F32R)
        w1tmp = sb("w1tmp", [P, FF])
        b1c = sb("b1c", [P, E * FC])
        w2 = sb("w2", [P, E * FC, D])
        b2 = sb("b2", [E, D])
        ident = sb("ident", [P, P])
        ident_r = sb("ident_r", [P, P], F32R)
        iota = sb("iota", [P, E])
        ropeA = sb("ropeA", [P, 3, TT, H, HD])
        ropeB = sb("ropeB", [P, 3, TT, H, HD])
        halves = sb("halves", [P, 2 * TT])
        ones = sb("ones", [P, P])

        stats = sb("stats", [P, TT, 6])
        meanvar = sb("meanvar", [P, TT, 2])
        vareps = sb("vareps", [P, TT])
        rstd = sb("rstd", [P, TT])
        stats2 = sb("stats2", [P, TT, 6])
        meanvar2 = sb("meanvar2", [P, TT, 2])
        vareps2 = sb("vareps2", [P, TT])
        rstd2 = sb("rstd2", [P, TT])
        stats3 = sb("stats3", [P, TT, 6])
        meanvar3 = sb("meanvar3", [P, TT, 2])
        vareps3 = sb("vareps3", [P, TT])
        rstd3 = sb("rstd3", [P, TT])
        Y = sb("Y", [P, TT, D])
        Z = sb("Z", [P, TT, D])
        ZT = sb("ZT", [P, T])
        QKV = sb("QKV", [P, 3, TT, D])
        R1 = sb("R1", [P, 3, TT, H, HD])
        R2 = sb("R2", [P, 3, TT, H, HD])
        R = sb("R", [P, 3, TT, D])
        hsum = sb("hsum", [P, 2 * TT * H])
        hmean = sb("hmean", [P, 2 * TT * H])
        hsq = sb("hsq", [P, 2 * TT * H])
        Qst = sb("Qst", [P, TT, H, SL], F32R)
        Kst = sb("Kst", [P, TT, H, SL], F32R)
        QT0 = sb("QT0", [P, NG, T], F32R)
        KT0 = sb("KT0", [P, NG, T], F32R)
        QT = sb("QT", [P, NG, T], F32R)
        KT = sb("KT", [P, NG, T], F32R)
        M = sb("M", [P, H, TT])
        Vmid = sb("Vmid", [P, TT, D])
        Vx = sb("Vx", [P, TT, H, SL])
        Pr = sb("Pr", [P, 2, HG, TT, T])
        OT = sb("OT", [P, NG, T])
        rden = sb("rden", [P, TT, H])
        On = sb("On", [P, TT, D])
        O1 = sb("O1", [P, TT, H, HD])
        O2 = sb("O2", [P, TT, H, HD])
        Or = sb("Or", [P, TT, D])
        OnT = sb("OnT", [P, T])
        U = sb("U", [P, TT, D])
        UT = sb("UT", [P, T])
        TH = sb("TH", [P, NB, T], F32R)
        TL = sb("TL", [P, NB, T], F32R)
        G = sb("G", [P, 2, FC, BLK])
        w1raw = G[:].rearrange("p a c n -> p (a c n)").rearrange("p (e f) -> p e f", e=E)
        LG = sb("LG", [P, NB, TT * E])
        lg = LG[:].rearrange("p b (t e) -> p (b t) e", e=E)
        pe_ = sb("pe_", [P, NT, E])
        col = sb("col", [P, NT])
        col2 = sb("col2", [P, NT])
        top = sb("top", [P, NT, E])
        idx = sb("idx", [P, NT, E], U32)
        pick = sb("pick", [P, NT, E])
        WE = sb("WE", [P, NT, E])
        WT = sb("WT", [E, NT, P])

        bankE = ctx.enter_context(nc.psum_tensor("bankE", [P, HG, TT, T], F32))
        bankO = ctx.enter_context(nc.psum_tensor("bankO", [P, 512], F32))
        bankA = ctx.enter_context(nc.psum_tensor("bankA", [P, 512], F32))
        bankB = ctx.enter_context(nc.psum_tensor("bankB", [P, 512], F32))
        bankC = ctx.enter_context(nc.psum_tensor("bankC", [P, 512], F32))
        front_bank = [bankB, bankA]

        in_x0 = sem("in_x0")
        in_x = sem("in_x")
        in_rope = sem("in_rope")
        in_cov = sem("in_cov")
        in_ffn = sem("in_ffn")
        in_moe = sem("in_moe")
        out_done = sem("out_done")
        primed_all = sem("primed_all")
        ffn_only = {"ffn": 1}
        norm_stats = event("norm_stats", 4)
        norm_rstd = event("norm_rstd", 2)
        normed = event("normed", 2)
        norm2_stats = event("norm2_stats", {"ffn": 4})
        norm2_rstd = event("norm2_rstd", {"ffn": 2})
        normed2 = event("normed2", {"ffn": 2})
        res_base = event("res_base", {"rope": 1, "ffn": 1})
        zT = event("zT", 1)
        zT_copied = event("zT_copied", 1)
        proj = event("proj", 2)
        proj_copied = event("proj_copied", 2)
        roped = event("roped", {"rope": 3})
        centred = event("centred", {"cov": 5})
        k_stacked = event("k_stacked", {"rope": 2, "ffn": 2, "cov": 4})
        q_stacked = event("q_stacked", {"rope": 3, "ffn": 3, "cov": 5})
        k_kept = event("k_kept", 1)
        v_mid = event("v_mid", 1)
        consts_set = sem("consts_set")
        cleared = sem("cleared")
        stackT = event("stackT", 4)
        stackT_copied = event("stackT_copied", 4)
        raw_scores = event("raw_scores", H)
        maxed = event("maxed", H)
        shifted = event("shifted", 1)
        shiftT = event("shiftT", 2)
        shiftT_copied = event("shiftT_copied", 2)
        scores = event("scores", 2 * NG)
        exped = event("exped", 2 * NG)
        pv = event("pv", NG)
        pv_copied = event("pv_copied", NG)
        v_ready = event("v_ready", 1)
        outT = event("outT", 2)
        divided = event("divided", 4)
        unroped = event("unroped", {"rope": 3})
        onT = event("onT", 1)
        onT_copied = event("onT_copied", 1)
        wo = event("wo", 1)
        res = event("res", 1)
        w1_split = event("w1_split", {"rope": 3})
        xh = event("xh", ffn_only)
        norm3_stats = event("norm3_stats", {"ffn": 4})
        norm3_rstd = event("norm3_rstd", {"ffn": 2})
        normed3 = event("normed3", {"ffn": 2})
        uT = event("uT", ffn_only)
        uT_copied = event("uT_copied", ffn_only)
        uT_split = event("uT_split", {"ffn": 2})
        gate = event("gate", ffn_only)
        gate_copied = event("gate_copied", ffn_only)
        waits_met = sem("waits_met")
        vx_set = sem("vx_set")
        setup_dve = sem("setup_dve")
        setup_pe = sem("setup_pe")
        gated = sem("gated")
        gate_exp = sem("gate_exp")
        hid = sem("hid")
        hid_act = sem("hid_act")
        expert = sem("expert")
        mixed = sem("mixed")
        weT = sem("weT")
        weT_copied = sem("weT_copied")
        b2mix = sem("b2mix")
        b2_added = sem("b2_added")
        primed += [hid_act, expert, mixed]
        NGATE = 14 + 2 * NT

        def as32(ap):
            return ap.bitcast(F32)

        def banks(b):
            return front_bank[b % 2]

        def apart(eng):
            eng.sem_inc(waits_met, 1)

        block = ctx.enter_context(nc.Block())

        def through(eng, layer, step):
            with eng.Fori(0, NB - 3) as i:
                step(*[(layer, Seq(i, r)) for r in range(4)])

        def program(eng, step, before_ffn, mixture):
            first = 0
            for ph in range(2):
                first, last = 2 * ph, 2 * ph + 1
                step(None, None, None, (first, 0))
                step(None, None, (first, 0), (first, 1))
                step(None, (first, 0), (first, 1), (first, 2))
                through(eng, first, step)
                before_ffn(last)
                step((first, NB - 3), (first, NB - 2), (first, NB - 1), (last, 0))
                step((first, NB - 2), (first, NB - 1), (last, 0), (last, 1))
                step((first, NB - 1), (last, 0), (last, 1), (last, 2))
                through(eng, last, step)
                step((last, NB - 3), (last, NB - 2), (last, NB - 1), None)
                step((last, NB - 2), (last, NB - 1), None, None)
                step((last, NB - 1), None, None, None)
                mixture(last, ph)

        @block.sync
        def _(sp):
            xin = d["x"].rearrange("b (t p) d -> p b t d", p=P)
            for b in range(NB):
                sp.dma_start(X[:, b], xin[:, b]).then_inc(in_x if b else in_x0, 16)
            for s in primed:
                sp.sem_inc(s, 1)
            sp.sem_inc(primed_all, 1)
            sp.dma_start(w_gate[:], d["w_gate"]).then_inc(in_ffn, 16)
            sp.dma_start(w_qkv["ffn"][:], d["w_qkv_ffn"]).then_inc(in_ffn, 16)
            sp.dma_start(w_o["ffn"][:], d["w_o_ffn"]).then_inc(in_ffn, 16)
            sp.dma_start(b_qkv["ffn"][:], d["b_qkv_ffn"]).then_inc(in_ffn, 16)
            sp.dma_start(b_o["ffn"][:], d["b_o_ffn"]).then_inc(in_ffn, 16)
            sp.dma_start(lncols[:], d["lncols"]).then_inc(in_ffn, 16)
            sp.dma_start(b1c[:], d["b1c"]).then_inc(in_ffn, 16)
            sp.dma_start(w1raw, d["w1"].rearrange("e p f -> p e f")).then_inc(in_ffn, 16)
            sp.dma_start(w_qkv["cov"][:], d["w_qkv_cov"]).then_inc(in_cov, 16)
            sp.dma_start(w_o["cov"][:], d["w_o_cov"]).then_inc(in_cov, 16)
            sp.dma_start(w2[:], d["w2"].rearrange("e (c p) d -> p (e c) d", p=P)).then_inc(in_moe, 16)
            sp.dma_start(b2[:], d["b2"]).then_inc(in_moe, 16)
            sp.dma_start(iota[:], d["iota"]).then_inc(in_moe, 16)
            sp.wait_ge(b2_added, 8)
            sp.dma_start(out.rearrange("b (t p) d -> p b t d", p=P), X[:]).then_inc(out_done, 16)
            sp.wait_ge(out_done, 16)

        @block.tensor
        def _(pe):
            pe.wait_ge(primed_all, 1)
            mm = nc.tensor.matmul

            def do_scores(layer, b, g, pair):
                need(pe, shiftT_copied, layer, b)
                need(pe, k_kept, layer, b)
                need(pe, exped, layer, b, 2 * g + pair - 1)
                for j in (2 * pair, 2 * pair + 1):
                    rows = slice(SL * j, SL * j + SL)
                    for kc in range(TT):
                        m = mm(bankE[:, j, kc], KT[rows, g, kc * P:kc * P + P], QT[rows, g, :],
                               start=True, stop=True)
                m.then_inc(scores.sem, 1)

            def do_pv(layer, b, g, kc):
                if kc == 0:
                    need(pe, exped, layer, b, 2 * g + 2)
                    need(pe, pv_copied, layer, b, g)
                    if g == 0:
                        need(pe, v_ready, layer, b)
                for j in range(HG):
                    rows = slice(SL * j, SL * j + SL)
                    m = mm(bankO[rows, 0:T], Vx[:, kc, HG * g + j, :], Pr[:, g % 2, j, kc, :],
                           start=(kc == 0), stop=(kc == TT - 1))
                if kc == TT - 1:
                    m.then_inc(pv.sem, 1)

            def do_zT(m, n):
                layer, b = n
                need(pe, normed2 if LAYERS[layer] == "ffn" else normed, layer, b)
                if m is not None:
                    need(pe, maxed, *m, 4)
                else:
                    need(pe, stackT_copied, layer, b, 0)
                for t in range(TT):
                    k = nc.tensor.transpose(bankA[:, t * P:t * P + P], Z[:, t, :], ident[:])
                k.then_inc(zT.sem, 1)

            def do_proj(m, n, t):
                layer, b = n
                need(pe, zT_copied, layer, b)
                if m is not None:
                    need(pe, maxed, *m, 5 + t)
                mm(banks(t)[:, 0:3 * D], ZT[:, t * P:t * P + P], w_qkv[LAYERS[layer]][:],
                   start=True, stop=True).then_inc(proj.sem, 1)

            def transpose_stack(dst, src, t):
                for g in range(NG):
                    k = mm(dst[:, g * P:g * P + P],
                           src[:, t, HG * g:HG * g + HG, :].rearrange("p h s -> p (h s)"), ident_r[:],
                           start=True, stop=True)
                return k

            def do_stackT(m, n, u):
                need(pe, k_stacked if u < 2 else q_stacked, *n)
                if m is None:
                    if u < 2:
                        need(pe, proj_copied, *n)
                    else:
                        need(pe, stackT_copied, *n, u - 1)
                elif u < 2:
                    need(pe, maxed, *m, H - 1 + u)
                else:
                    need(pe, shiftT_copied, *m, u - 1)
                transpose_stack(banks(u), Kst if u < 2 else Qst, u % 2).then_inc(stackT.sem, 1)

            def do_raw(m, n, h):
                if h < 2:
                    need(pe, stackT_copied, *m)
                elif h == 5 and n is not None:
                    need(pe, zT_copied, *n)
                elif h in (6, 7) and n is not None:
                    need(pe, proj_copied, *n, h - 5)
                else:
                    need(pe, maxed, *m, h - 1)
                g, j = h // HG, h % HG
                rows = slice(SL * j, SL * j + SL)
                for t in range(TT):
                    k = mm(banks(h)[:, t * T:t * T + T], QT0[rows, g, t * P:t * P + P], KT0[rows, g, :],
                           start=True, stop=True)
                k.then_inc(raw_scores.sem, 1)

            def do_shiftT(m, n, t):
                if n is not None:
                    need(pe, stackT_copied, *n, t + 1)
                else:
                    need(pe, maxed, *m)
                need(pe, shifted, *m)
                transpose_stack(banks(t), Qst, t).then_inc(shiftT.sem, 1)

            def do_outT(layer, b, t):
                if t == 0:
                    need(pe, pv_copied, layer, b)
                    need(pe, res, layer, b, 0)
                    need(pe, gate_copied, layer, b, 0)
                else:
                    need(pe, divided, layer, b, 2 * t)
                for g in range(NG):
                    m = nc.tensor.transpose(bankC[:, g * P:g * P + P], OT[:, g, t * P:t * P + P], ident[:])
                m.then_inc(outT.sem, 1)

            def do_onT(layer, b):
                kind = LAYERS[layer]
                need(pe, divided, layer, b)
                if kind == "rope":
                    need(pe, unroped, layer, b)
                src = Or if kind == "rope" else On
                for t in range(TT):
                    m = nc.tensor.transpose(bankC[:, t * P:t * P + P], src[:, t, :], ident[:])
                m.then_inc(onT.sem, 1)

            def do_wo(layer, b):
                kind = LAYERS[layer]
                need(pe, onT_copied, layer, b)
                for t in range(TT):
                    m = mm(bankC[:, t * D:t * D + D], OnT[:, t * P:t * P + P], w_o[kind][:], start=True, stop=True)
                m.then_inc(wo.sem, 1)

            def do_uT(layer, b):
                if LAYERS[layer] == "ffn":
                    need(pe, res, layer, b)
                    need(pe, normed3, layer, b)
                    for t in range(TT):
                        m = nc.tensor.transpose(bankC[:, t * P:t * P + P], U[:, t, :], ident[:])
                    m.then_inc(uT.sem, 1)

            def do_gate(layer, b):
                if LAYERS[layer] == "ffn":
                    need(pe, uT_copied, layer, b)
                    for t in range(TT):
                        m = mm(bankC[:, t * E:t * E + E], UT[:, t * P:t * P + P], w_gate_n[:], start=True, stop=True)
                    m.then_inc(gate.sem, 1)

            def step(t, a, m, n):
                def of(role, f, *args):
                    if role is not None:
                        f(*role, *args)

                def raw(*hs):
                    for h in hs:
                        if m is not None:
                            do_raw(m, n, h)

                def prep(f, *args):
                    if n is not None:
                        f(m, n, *args)

                raw(0, 1)
                of(t, do_onT)
                of(a, do_scores, 1, 0)
                raw(2)
                of(a, do_scores, 1, 1)
                of(a, do_pv, 0, 0)
                raw(3)
                of(t, do_wo)
                of(a, do_pv, 0, 1)
                raw(4)
                of(a, do_scores, 2, 0)
                prep(do_zT)
                of(a, do_scores, 2, 1)
                raw(5)
                prep(do_proj, 0)
                prep(do_proj, 1)
                raw(6)
                of(a, do_pv, 1, 0)
                raw(7)
                of(a, do_pv, 1, 1)
                of(t, do_uT)
                raw(8)
                of(a, do_scores, 3, 0)
                raw(9)
                of(a, do_scores, 3, 1)
                of(t, do_gate)
                of(a, do_pv, 2, 0)
                raw(10)
                of(a, do_pv, 2, 1)
                raw(11, 12, 13)
                of(a, do_pv, 3, 0)
                raw(14)
                of(a, do_pv, 3, 1)
                raw(15)
                prep(do_stackT, 0)
                prep(do_stackT, 1)
                if m is not None:
                    do_shiftT(m, n, 0)
                    do_shiftT(m, n, 1)
                of(a, do_outT, 0)
                prep(do_stackT, 2)
                prep(do_stackT, 3)
                of(a, do_outT, 1)
                of(m, do_scores, 0, 0)
                of(m, do_scores, 0, 1)

            def setup_ffn():
                pe.wait_ge(in_ffn, 8 * 16)
                pe.wait_ge(setup_dve, 2)
                need(pe, divided, 0, NB - 3)
                need(pe, pv_copied, 0, NB - 3)
                mm(bankC[:, 0:3 * D], lnb[:, 0, :], w_qkv["ffn"][:], start=True, stop=True).then_inc(setup_pe, 1)
                for n in range(E * FC):
                    mm(bankO[:, n:n + 1], w1raw[:, n // FC, (n % FC) * P:(n % FC) * P + P], lncols[:, 3:4],
                       start=True, stop=True)
                mm(bankO[:, 64:64 + E], lnb[:, 1, :], w_gate[:], start=True, stop=True).then_inc(setup_pe, 1)
                pe.wait_ge(setup_dve, 7)

            def mixture(layer, ph):
                need(pe, uT_split, layer, NB - 1)
                need(pe, exped, layer, NB - 1)
                if ph == 0:
                    pe.wait_ge(in_moe, 3 * 16)
                need(pe, w1_split, layer, 0, 0)

                def hidden(j, e):
                    for c in range(FC):
                        base = ph * NBLK * E * FC + e * FC + c - FC + 1
                        v = j * (E * FC) + (base + 1)
                        if e or ph:
                            pe.wait_ge(hid_act, v)
                        else:
                            pe.wait_ge(hid_act, j * (E * FC) + 1)
                        w = slice(c * P, c * P + P)
                        n = (e * FC + c) % 4
                        acc = bankE[:, n].rearrange("p k q -> p (k q)")
                        th = TH[:].rearrange("p b t -> p (b t)").rearrange("p (j n) -> p j n", j=NBLK)[:, j]
                        tl = TL[:].rearrange("p b t -> p (b t)").rearrange("p (j n) -> p j n", j=NBLK)[:, j]
                        mm(acc, w1h[:, e, w], th, start=True, stop=False)
                        mm(acc, w1h[:, e, w], tl, start=False, stop=False)
                        mm(acc, w1l[:, e, w], th, start=False, stop=True).then_inc(hid, 1)

                def outputs(j, e):
                    pe.wait_ge(hid_act, j * (E * FC) + (ph * NBLK * E * FC + (e + 1) * FC + 1))
                    if e >= 2 or ph:
                        pe.wait_ge(mixed, j * (E * BT) + (ph * NBLK * E * BT + (e - 1) * BT + 1))
                    else:
                        pe.wait_ge(mixed, j * (E * BT) + 1)
                    for t in range(BT):
                        for c in range(FC):
                            m = mm(banks(e)[:, t * D:t * D + D], G[:, e % 2, c, t * P:t * P + P],
                                   w2[:, e * FC + c, :], start=(c == 0), stop=(c == FC - 1))
                    m.then_inc(expert, 1)

                with pe.Fori(0, NBLK) as j:
                    hidden(j, 0)
                    for e in range(E):
                        if e + 1 < E:
                            hidden(j, e + 1)
                        outputs(j, e)

                pe.wait_ge(gated, (ph + 1) * NGATE)
                need(pe, gate_copied, layer, NB - 1)
                need(pe, pv_copied, layer, NB - 1)
                wb = [bankC, bankO]
                for q in range(4):
                    if q >= 2:
                        pe.wait_ge(weT_copied, 4 * ph + q - 1)
                    for t in range(4):
                        m = nc.tensor.transpose(wb[q % 2][0:E, t * P:t * P + P], WE[:, 4 * q + t, :], ident[:])
                    m.then_inc(weT, 1)
                for q in range(4):
                    if q < 2:
                        pe.wait_ge(weT_copied, 4 * ph + 3 + q)
                    else:
                        pe.wait_ge(b2_added, 4 * ph + q - 1)
                    for t in range(4):
                        m = mm(wb[q % 2][:, t * D:t * D + D], WT[:, 4 * q + t, :], b2[:], start=True, stop=True)
                    m.then_inc(b2mix, 1)

            def before_ffn(layer):
                if layer == 1:
                    setup_ffn()

            def mixture_then(layer, ph):
                mixture(layer, ph)
                if ph == 0:
                    pe.wait_ge(in_cov, 2 * 16)
                    pe.wait_ge(mixed, NBLK * E * BT + 1)
                    pe.wait_ge(b2_added, 4)
                    pe.wait_ge(hid_act, NBLK * E * FC + 1)

            pe.wait_ge(in_rope, 6 * 16)
            pe.wait_ge(vx_set, 3)
            pe.wait_ge(consts_set, 5)
            program(pe, step, before_ffn, mixture_then)

        @block.scalar
        def _(act):
            act.dma_start(w_qkv["rope"][:], d["w_qkv_rope"]).then_inc(in_rope, 16)
            act.dma_start(ident[:], d["ident"]).then_inc(in_rope, 16)
            act.dma_start(b_qkv["rope"][:], d["b_qkv_rope"]).then_inc(in_rope, 16)
            act.dma_start(ropeA[:], d["ropeA"]).then_inc(in_rope, 16)
            act.dma_start(ropeB[:], d["ropeB"]).then_inc(in_rope, 16)
            act.dma_start(w_o["rope"][:], d["w_o_rope"]).then_inc(in_rope, 16)
            act.dma_start(b_o["rope"][:], d["b_o_rope"]).then_inc(in_rope, 16)
            act.wait_ge(primed_all, 1)

            def copy(dst, src):
                return nc.scalar.activation(dst, src, ACT.Copy)

            def do_exp(layer, b, g, pair):
                need(act, scores, layer, b, 2 * g + pair + 1)
                need(act, pv, layer, b, g - 1)
                js = slice(2 * pair, 2 * pair + 2)
                nc.scalar.activation(Pr[:, g % 2, js], bankE[:, js], ACT.Exp,
                                     scale=EXP_SCALE[LAYERS[layer]]).then_inc(exped.sem, 1)

            def do_zT(layer, b):
                need(act, zT, layer, b)
                need(act, proj, layer, b, 0)
                copy(ZT[:], bankA[:, 0:T]).then_inc(zT_copied.sem, 1)

            def do_pv(layer, b, g):
                need(act, pv, layer, b, g + 1)
                if g == 0:
                    need(act, outT, layer, b, 0)
                copy(OT[:, g, :], bankO[:, 0:T]).then_inc(pv_copied.sem, 1)

            def do_stackT(layer, b, u):
                dst = KT0 if u < 2 else QT0
                need(act, stackT, layer, b, u + 1)
                if u == 0:
                    need(act, raw_scores, layer, b, 0)
                    need(act, k_kept, layer, b, 0)
                copy(dst[:, :, (u % 2) * P:(u % 2) * P + P],
                     banks(u)[:].rearrange("p (g t) -> p g t", g=NG)).then_inc(stackT_copied.sem, 1)

            def do_shiftT(layer, b):
                for t in range(TT):
                    need(act, shiftT, layer, b, t + 1)
                    if t == 0:
                        need(act, scores, layer, b, 0)
                    copy(QT[:, :, t * P:t * P + P],
                         banks(t)[:].rearrange("p (g t) -> p g t", g=NG)).then_inc(shiftT_copied.sem, 1)

            def do_onT(layer, b):
                need(act, onT, layer, b)
                need(act, wo, layer, b, 0)
                copy(OnT[:], bankC[:, 0:T]).then_inc(onT_copied.sem, 1)

            def do_uT(layer, b):
                if LAYERS[layer] == "ffn":
                    need(act, uT, layer, b)
                    need(act, gate, layer, b, 0)
                    need(act, uT_split, layer, b, 0)
                    copy(UT[:], bankC[:, 0:T]).then_inc(uT_copied.sem, 1)

            def do_gate(layer, b):
                if LAYERS[layer] == "ffn":
                    need(act, gate, layer, b)
                    copy(LG[:, at(b), :], bankC[:, 0:TT * E]).then_inc(gate_copied.sem, 1)

            def step(t, a, m, n):
                def of(role, f, *args):
                    if role is not None:
                        f(*role, *args)

                of(t, do_onT)
                of(a, do_exp, 1, 0)
                of(a, do_exp, 1, 1)
                of(a, do_pv, 0)
                of(n, do_zT)
                of(a, do_exp, 2, 0)
                of(a, do_exp, 2, 1)
                of(a, do_pv, 1)
                of(t, do_uT)
                of(a, do_exp, 3, 0)
                of(a, do_exp, 3, 1)
                of(t, do_gate)
                of(a, do_pv, 2)
                of(a, do_pv, 3)
                of(n, do_stackT, 0)
                of(n, do_stackT, 1)
                of(m, do_shiftT)
                of(n, do_stackT, 2)
                of(n, do_stackT, 3)
                of(m, do_exp, 0, 0)
                of(m, do_exp, 0, 1)

            def mixture(layer, ph):
                act.wait_ge(gated, ph * NGATE + 3)
                nc.scalar.activation(pe_[:], lg, ACT.Exp).then_inc(gate_exp, 1)
                need(act, pv, layer, NB - 1)
                with act.Fori(0, NBLK) as j:
                    for e in range(E):
                        if e >= 2 or ph:
                            act.wait_ge(expert, j * E + (ph * NBLK * E + e - 1 + 1))
                        else:
                            act.wait_ge(expert, j * E + 1)
                        for c in range(FC):
                            act.wait_ge(hid, j * (E * FC) + (ph * NBLK * E * FC + e * FC + c + 1))
                            n = (e * FC + c) % 4
                            nc.scalar.activation(G[:, e % 2, c, :], bankE[:, n].rearrange("p k q -> p (k q)"),
                                                 ACT.Gelu_apprx_tanh,
                                                 bias=b1c[:, e * FC + c:e * FC + c + 1]).then_inc(hid_act, 1)
                for q in range(4):
                    act.wait_ge(weT, 4 * ph + q + 1)
                    if q == 0 and ph:
                        act.wait_ge(b2mix, 4 * ph)
                    wb = [bankC, bankO][q % 2]
                    copy(WT[:, 4 * q:4 * q + 4, :], wb[0:E, :].rearrange("e (t p) -> e t p", t=4)).then_inc(weT_copied, 1)

            program(act, step, lambda layer: None, mixture)

        @block.vector
        def _(dve):
            dve.wait_ge(primed_all, 1)
            v = nc.vector
            tt = v.tensor_tensor

            def stats_of(layer, b, ev, src, st, mv):
                apart(dve)
                for t in range(TT):
                    v.bn_stats(st[:, t, :], src[:, t, :]).then_inc(ev.sem, 1)
                for t in range(TT):
                    need(dve, ev, layer, b, t + 1)
                    apart(dve)
                    v.bn_aggr(mv[:, t, :], st[:, t, :]).then_inc(ev.sem, 1)

            def normalise(layer, b, ev, dst, src, mv, rs):
                for t in range(TT):
                    v.tensor_scalar(dst[:, t, :], src[:, t, :], mv[:, t, 0:1], rs[:, t:t + 1],
                                    ALU.subtract, ALU.mult).then_inc(ev.sem, 1)

            def norm_in(layer, b):
                if layer == 0:
                    if isinstance(b, int) and b == 0:
                        dve.wait_ge(in_x0, 16)
                    else:
                        dve.wait_ge(in_x, (NB - 1) * 16)
                elif LAYERS[layer] != "ffn":
                    dve.wait_ge(b2_added, 4 * (layer // 2))
                else:
                    need(dve, res, layer - 1, b)
                stats_of(layer, b, norm_stats, X[:, at(b)], stats, meanvar)

            def norm_out(layer, b):
                ffn = LAYERS[layer] == "ffn"
                need(dve, norm_rstd, layer, b)
                if ffn:
                    need(dve, res_base, layer, b, 0)
                else:
                    need(dve, zT, layer, b, 0)
                normalise(layer, b, normed, Y if ffn else Z, X[:, at(b)], meanvar, rstd)
                if ffn:
                    need(dve, normed, layer, b)
                    stats_of(layer, b, norm2_stats, Y, stats2, meanvar2)

            def norm2_out(layer, b):
                if LAYERS[layer] == "ffn":
                    need(dve, norm2_rstd, layer, b)
                    need(dve, zT, layer, b, 0)
                    normalise(layer, b, normed2, Z, Y, meanvar2, rstd2)

            def do_proj(layer, b, t):
                kind = LAYERS[layer]
                need(dve, v_mid, layer, b, 0)
                need(dve, proj, layer, b, t + 1)
                src = banks(t)[:, 0:3 * D].rearrange("p (c d) -> p c d", c=3)
                if kind == "cov":
                    v.tensor_copy(QKV[:, :, t, :], src).then_inc(proj_copied.sem, 1)
                else:
                    tt(QKV[:, :, t, :], src, b_qkv[kind][:], ALU.add).then_inc(proj_copied.sem, 1)

            def heads(ap):
                return ap.rearrange("p c t (h x) -> p (c t h) x", x=HD)

            def rope_operands(ap):
                half = ap.rearrange("p n (w o) -> p n w o", o=2)
                n = ap.shape[1]
                ev = half[:, :, :, 0].unsqueeze(2).broadcast_to([P, n, 2, HD // 2])
                od = half[:, :, :, 1].unsqueeze(2).broadcast_to([P, n, 2, HD // 2])
                return ev, od

            def flat(ap):
                return ap.rearrange("p c t h (u w) -> p (c t h) u w", u=2)

            def rope(layer, b, part):
                ev, od = rope_operands(heads(QKV[:]))
                if part == 0:
                    need(dve, proj_copied, layer, b)
                    tt(flat(R1[:]), ev, flat(ropeA[:]), ALU.mult).then_inc(roped.sem, 1)
                elif part == 1:
                    tt(flat(R2[:]), od, flat(ropeB[:]), ALU.mult).then_inc(roped.sem, 1)
                else:
                    need(dve, roped, layer, b, 2)
                    tt(heads(R[:]), R1[:].rearrange("p c t h x -> p (c t h) x"),
                       R2[:].rearrange("p c t h x -> p (c t h) x"), ALU.add).then_inc(roped.sem, 1)

            def centre(layer, b, part):
                n = 2 * TT * H
                qk = heads(QKV[:, 0:2])
                dst = heads(R[:, 0:2])
                sq = R1[:, 0:2].rearrange("p c t h x -> p (c t h) x")
                if part == 0:
                    need(dve, proj_copied, layer, b)
                    v.tensor_reduce(hsum[:], qk, AX.X, ALU.add).then_inc(centred.sem, 1)
                    need(dve, centred, layer, b, 1)
                    v.tensor_scalar(hmean[:], hsum[:], 1.0 / HD, None, ALU.mult).then_inc(centred.sem, 1)
                elif part == 1:
                    need(dve, centred, layer, b, 2)
                    tt(dst, qk, hmean[:].unsqueeze(2).broadcast_to([P, n, HD]), ALU.subtract).then_inc(centred.sem, 1)
                else:
                    need(dve, centred, layer, b, 3)
                    tt(sq, dst, dst, ALU.mult).then_inc(centred.sem, 1)
                    need(dve, centred, layer, b, 4)
                    v.tensor_reduce(hsq[:], sq, AX.X, ALU.add).then_inc(centred.sem, 1)

            def turn(layer, b, part):
                if LAYERS[layer] == "rope":
                    rope(layer, b, part)
                elif LAYERS[layer] == "cov":
                    centre(layer, b, part)

            def stack_operand(layer, c):
                kind = LAYERS[layer]
                src = QKV if kind == "ffn" else R
                return src[:, c].rearrange("p t (h x) -> p (t h) x", x=HD)

            STH = TT * H
            INV = 1.0 / (HD - 1)

            def twice(ap):
                return ap.unsqueeze(2).broadcast_to([P, STH, 2, HD])

            cleared_count = [0]

            def clear(stack, layer, b):
                if layer == 3 and isinstance(b, int) and b == 0:
                    v.memset(as32(stack[:, :, 3 * HD:SHIFT]), 0.0).then_inc(cleared, 1)
                    cleared_count[0] += 1
                    dve.wait_ge(cleared, cleared_count[0])

            def stack_k(layer, b, part):
                kind = LAYERS[layer]
                k = stack_operand(layer, 1)
                ks = Kst[:].rearrange("p t h s -> p (t h) s")
                hk = hsq[:, STH:2 * STH].unsqueeze(2)
                if part == 0:
                    need(dve, {"ffn": proj_copied, "rope": roped, "cov": centred}[kind], layer, b)
                    need(dve, stackT, layer, b, 0)
                    clear(ks, layer, b)
                    k_hi = ks[:, :, 0:4 * HD].rearrange("p n (r y) -> p n r y", r=2)[:, :, :, 0:HD]
                    v.tensor_copy(k_hi, twice(k)).then_inc(k_stacked.sem, 1)
                    if kind == "cov":
                        v.tensor_scalar(ks[:, :, 24:28].rearrange("p n (r y) -> p n r y", y=2)[:, :, :, 0],
                                        hk.broadcast_to([P, STH, 2]), INV, None, ALU.mult).then_inc(k_stacked.sem, 1)
                else:
                    need(dve, k_stacked, layer, b, 2 if kind == "cov" else 1)
                    tt(ks[:, :, HD:2 * HD], k, as32(ks[:, :, 0:HD]), ALU.subtract).then_inc(k_stacked.sem, 1)
                    if kind == "cov":
                        v.scalar_tensor_tensor(ks[:, :, 25:26], hk, INV, as32(ks[:, :, 24:25]),
                                               ALU.mult, ALU.subtract).then_inc(k_stacked.sem, 1)

            def stack_q(layer, b):
                kind = LAYERS[layer]
                q = stack_operand(layer, 0)
                qs = Qst[:].rearrange("p t h s -> p (t h) s")
                hq = hsq[:, 0:STH].unsqueeze(2)
                need(dve, {"ffn": proj_copied, "rope": roped, "cov": centred}[kind], layer, b)
                need(dve, shiftT, layer, b, 0)
                clear(qs, layer, b)
                v.tensor_copy(qs[:, :, 0:2 * HD].rearrange("p n (r x) -> p n r x", r=2),
                              twice(q)).then_inc(q_stacked.sem, 1)
                v.memset(as32(qs[:, :, SHIFT:SHIFT + 1]), 0.0).then_inc(q_stacked.sem, 1)
                if kind == "cov":
                    v.tensor_scalar(qs[:, :, 24:26], hq.broadcast_to([P, STH, 2]), INV, None,
                                    ALU.mult).then_inc(q_stacked.sem, 1)
                need(dve, q_stacked, layer, b, 3 if kind == "cov" else 1)
                tt(qs[:, :, 2 * HD:3 * HD], q, as32(qs[:, :, 0:HD]), ALU.subtract).then_inc(q_stacked.sem, 1)
                if kind == "cov":
                    v.scalar_tensor_tensor(qs[:, :, 26:27], hq, INV, as32(qs[:, :, 24:25]),
                                           ALU.mult, ALU.subtract).then_inc(q_stacked.sem, 1)

            def do_max(layer, b, h):
                need(dve, raw_scores, layer, b, h + 1)
                v.tensor_reduce(M[:, h, :], banks(h)[:].rearrange("p (t k) -> p t k", t=TT),
                                AX.X, ALU.max).then_inc(maxed.sem, 1)

            def shift(layer, b):
                need(dve, maxed, layer, b)
                need(dve, stackT, layer, b)
                v.tensor_scalar(Qst[:, :, :, SHIFT], M[:].rearrange("p h t -> p t h"), -1.0, None,
                                ALU.mult).then_inc(shifted.sem, 1)

            def divide(layer, b, t):
                need(dve, outT, layer, b, t + 1)
                if t == 0:
                    need(dve, onT, layer, b, 0)
                o = bankC[:].rearrange("p (h s) -> p h s", s=SL)
                v.reciprocal(rden[:, t, :], o[:, :, HD]).then_inc(divided.sem, 1)
                need(dve, divided, layer, b, 2 * t + 1)
                tt(On[:, t, :].rearrange("p (h x) -> p h x", x=HD), o[:, :, 0:HD],
                   rden[:, t, :].unsqueeze(2).broadcast_to([P, H, HD]), ALU.mult).then_inc(divided.sem, 1)

            def unrope(layer, b):
                need(dve, divided, layer, b)
                ev, od = rope_operands(On[:].rearrange("p t (h x) -> p (t h) x", x=HD))
                f = lambda ap: ap.rearrange("p t h (u w) -> p (t h) u w", u=2)
                tt(f(O1[:]), ev, f(ropeA[:, 0]), ALU.mult).then_inc(unroped.sem, 1)
                tt(f(O2[:]), od, f(ropeB[:, 0]), ALU.mult).then_inc(unroped.sem, 1)
                need(dve, unroped, layer, b, 2)
                need(dve, onT, layer, b, 0)
                v.scalar_tensor_tensor(Or[:].rearrange("p t d -> p (t d)"), O1[:].rearrange("p t h x -> p (t h x)"),
                                       -1.0, O2[:].rearrange("p t h x -> p (t h x)"),
                                       ALU.mult, ALU.subtract).then_inc(unroped.sem, 1)

            def residual(layer, b):
                kind = LAYERS[layer]
                need(dve, wo, layer, b)
                if kind != "cov":
                    need(dve, res_base, layer, b)
                dst = Hs if kind == "ffn" else X
                tt(dst[:, at(b)], bankC[:, 0:T].rearrange("p (t d) -> p t d", t=TT), dst[:, at(b)],
                   ALU.add).then_inc(res.sem, 1)

            def norm3_in(layer, b):
                if LAYERS[layer] == "ffn":
                    need(dve, res, layer, b)
                    stats_of(layer, b, norm3_stats, Hs[:, at(b)], stats3, meanvar3)

            def norm3_out(layer, b):
                if LAYERS[layer] == "ffn":
                    need(dve, norm3_rstd, layer, b)
                    need(dve, uT, layer, b, 0)
                    normalise(layer, b, normed3, U, Hs[:, at(b)], meanvar3, rstd3)

            def unrope_if(layer, b):
                if LAYERS[layer] == "rope":
                    unrope(layer, b)

            def step(t, a, m, n):
                def of(role, f, *args):
                    if role is not None:
                        f(*role, *args)

                of(m, do_max, 0)
                of(n, norm_in)
                of(m, do_max, 1)
                of(m, do_max, 2)
                of(n, norm_out)
                of(m, do_max, 3)
                of(t, residual)
                of(m, do_max, 4)
                of(n, norm2_out)
                of(t, norm3_in)
                of(m, do_max, 5)
                of(n, do_proj, 0)
                of(t, norm3_out)
                of(n, do_proj, 1)
                of(m, do_max, 6)
                of(m, do_max, 7)
                of(n, turn, 0)
                of(m, do_max, 8)
                of(n, turn, 1)
                of(m, do_max, 9)
                of(n, turn, 2)
                of(m, do_max, 10)
                of(n, stack_k, 0)
                of(m, do_max, 11)
                of(m, do_max, 12)
                of(n, stack_k, 1)
                of(m, do_max, 13)
                of(m, do_max, 14)
                of(m, do_max, 15)
                of(m, shift)
                of(a, divide, 0)
                of(n, stack_q)
                of(a, divide, 1)
                of(a, unrope_if)

            def setup_ffn():
                dve.wait_ge(in_ffn, 8 * 16)
                v.tensor_scalar(lnb[:, 0, :], ones[:], lncols[:, 1:2], None, ALU.mult).then_inc(setup_dve, 1)
                v.tensor_scalar(lnb[:, 1, :], ones[:], lncols[:, 3:4], None, ALU.mult).then_inc(setup_dve, 1)
                dve.wait_ge(setup_pe, 2)
                tt(b_qkv["ffn"][:], bankC[:, 0:3 * D].rearrange("p (c d) -> p c d", c=3), b_qkv["ffn"][:],
                   ALU.add).then_inc(setup_dve, 1)
                tt(b1c[:], bankO[:, 0:E * FC], b1c[:], ALU.add).then_inc(setup_dve, 1)
                v.tensor_copy(gate_bias[:], bankO[:, 64:64 + E]).then_inc(setup_dve, 1)
                v.tensor_scalar(w_qkv["ffn"][:], w_qkv["ffn"][:], lncols[:, 0:1], None,
                                ALU.mult).then_inc(setup_dve, 1)
                v.tensor_scalar(w_gate_n[:], w_gate[:], lncols[:, 2:3], None, ALU.mult).then_inc(setup_dve, 1)
                dve.wait_ge(setup_dve, 7)

            def mixture(layer, ph):
                done = [ph * NGATE]

                def then(ins):
                    ins.then_inc(gated, 1)
                    done[0] += 1
                    dve.wait_ge(gated, done[0])

                def across(c):
                    return c.unsqueeze(2).broadcast_to([P, NT, E])

                if ph == 0:
                    dve.wait_ge(in_moe, 3 * 16)
                need(dve, gate_copied, layer, NB - 1)
                then(tt(lg, lg, gate_bias[:].unsqueeze(1).broadcast_to([P, NT, E]), ALU.add))
                then(v.tensor_reduce(col[:], lg, AX.X, ALU.max))
                then(tt(lg, lg, across(col[:]), ALU.subtract))
                dve.wait_ge(gate_exp, ph + 1)
                then(v.tensor_reduce(col[:], pe_[:], AX.X, ALU.add))
                then(v.reciprocal(col2[:], col[:]))
                then(tt(pe_[:], pe_[:], across(col2[:]), ALU.mult))
                for t in range(NT):
                    then(v.max(top[:, t, :], pe_[:, t, :]))
                for t in range(NT):
                    then(v.max_index(idx[:, t, :], top[:, t, :], pe_[:, t, :]))
                then(tt(col[:], top[:, :, 0], top[:, :, 1], ALU.add))
                then(v.reciprocal(col2[:], col[:]))
                then(tt(top[:, :, 0:2], top[:, :, 0:2], col2[:].unsqueeze(2).broadcast_to([P, NT, 2]), ALU.mult))
                io = iota[:].unsqueeze(1).broadcast_to([P, NT, E])
                then(tt(pick[:], io, across(idx[:, :, 0]), ALU.is_equal))
                if ph:
                    dve.wait_ge(weT, 4 * ph)
                then(tt(WE[:], pick[:], across(top[:, :, 0]), ALU.mult))
                then(tt(pick[:], io, across(idx[:, :, 1]), ALU.is_equal))
                then(tt(pick[:], pick[:], across(top[:, :, 1]), ALU.mult))
                then(tt(WE[:], WE[:], pick[:], ALU.add))

                need(dve, xh, layer, NB - 1)
                xt = X[:].rearrange("p b t d -> p (b t) d").rearrange("p (j t) d -> p j t d", j=NBLK)
                we = WE[:].rearrange("p (j t) e -> p j t e", j=NBLK)
                with dve.Fori(0, NBLK) as j:
                    for e in range(E):
                        dve.wait_ge(expert, j * E + (ph * NBLK * E + e + 1 + 1))
                        for t in range(BT):
                            if e or ph:
                                dve.wait_ge(mixed, j * (E * BT) + (ph * NBLK * E * BT + (e - 1) * BT + t + 1 + 1))
                            v.scalar_tensor_tensor(xt[:, j, t, :], banks(e)[:, t * D:t * D + D],
                                                   we[:, j, t, e:e + 1], xt[:, j, t, :],
                                                   ALU.mult, ALU.add).then_inc(mixed, 1)
                dve.wait_ge(mixed, (ph + 1) * NBLK * E * BT + 1)
                for q in range(4):
                    dve.wait_ge(b2mix, 4 * ph + q + 1)
                    xq = X[:].rearrange("p b t d -> p (b t) d")[:, 4 * q:4 * q + 4, :]
                    tt(xq, [bankC, bankO][q % 2][:].rearrange("p (t d) -> p t d", t=4), xq,
                       ALU.add).then_inc(b2_added, 1)

            dve.wait_ge(in_rope, 7 * 16)
            dve.wait_ge(consts_set, 5)

            def before_ffn(layer):
                if layer == 1:
                    setup_ffn()

            program(dve, step, before_ffn, mixture)

        @block.gpsimd
        def _(pool):
            pool.wait_ge(primed_all, 1)
            g = nc.gpsimd
            g.memset(ones[:], 1.0).then_inc(consts_set, 1)
            g.memset(halves[:], -0.5).then_inc(consts_set, 1)
            g.memset(Vx[:], 0.0).then_inc(vx_set, 1)
            pool.wait_ge(vx_set, 1)
            g.memset(Vx[:, :, :, HD:HD + 1], 1.0).then_inc(vx_set, 1)
            pool.wait_ge(vx_set, 2)

            def power(layer, b, stats_ev, ev, mv, ve, rs, applied):
                need(pool, stats_ev, layer, b)
                need(pool, applied, layer, b, 0)
                apart(pool)
                g.tensor_scalar(ve[:], mv[:, :, 1], EPS, None, ALU.add).then_inc(ev.sem, 1)
                need(pool, ev, layer, b, 1)
                g.tensor_tensor(rs[:], ve[:], halves[:, 0:TT], ALU.pow).then_inc(ev.sem, 1)

            def norm_powers(layer, b):
                power(layer, b, norm_stats, norm_rstd, meanvar, vareps, rstd, normed)
                if LAYERS[layer] == "ffn":
                    power(layer, b, norm2_stats, norm2_rstd, meanvar2, vareps2, rstd2, normed2)

            def residual_base(layer, b):
                kind = LAYERS[layer]
                if kind != "cov":
                    need(pool, normed, layer, b)
                    src = Y[:] if kind == "ffn" else X[:, at(b)]
                    dst = Hs[:, at(b)] if kind == "ffn" else X[:, at(b)]
                    g.tensor_tensor(dst, src, b_o[kind][:].unsqueeze(1).broadcast_to([P, TT, D]),
                                    ALU.add).then_inc(res_base.sem, 1)

            def keep_k(layer, b):
                need(pool, stackT_copied, layer, b)
                need(pool, scores, layer, b, 0)
                apart(pool)
                g.tensor_copy(KT[:], as32(KT0[:])).then_inc(k_kept.sem, 1)

            def widen_v(layer, b):
                need(pool, v_mid, layer, b)
                need(pool, pv, layer, b, 0)
                apart(pool)
                g.tensor_copy(Vx[:, :, :, 0:HD].rearrange("p t h x -> p (t h) x"),
                              Vmid[:].rearrange("p t (h x) -> p (t h) x", x=HD)).then_inc(v_ready.sem, 1)

            def keep_v(layer, b):
                kind = LAYERS[layer]
                need(pool, roped if kind == "rope" else proj_copied, layer, b)
                need(pool, v_ready, layer, b, 0)
                apart(pool)
                src = R if kind == "rope" else QKV
                g.tensor_copy(Vmid[:], src[:, 2]).then_inc(v_mid.sem, 1)

            def split_w1(layer, b):
                if LAYERS[layer] != "rope":
                    return
                e = at(b)
                pool.wait_ge(in_ffn, 8 * 16)
                need(pool, w1_split, layer, b, 0)
                g.tensor_tensor(w1tmp[:], w1raw[:, e, :], lncols[:, 2:3].broadcast_to([P, FF]),
                                ALU.mult).then_inc(w1_split.sem, 1)
                need(pool, w1_split, layer, b, 1)
                apart(pool)
                g.tensor_copy(w1h[:, e, :], w1tmp[:]).then_inc(w1_split.sem, 1)
                need(pool, w1_split, layer, b, 2)
                g.tensor_tensor(w1l[:, e, :], w1tmp[:], as32(w1h[:, e, :]), ALU.subtract).then_inc(w1_split.sem, 1)

            def close_attention(layer, b):
                if LAYERS[layer] == "ffn":
                    need(pool, res, layer, b)
                    power(layer, b, norm3_stats, norm3_rstd, meanvar3, vareps3, rstd3, normed3)
                    g.tensor_tensor(X[:, at(b)], X[:, at(b)], Hs[:, at(b)], ALU.add).then_inc(xh.sem, 1)

            def split_u(layer, b):
                if LAYERS[layer] == "ffn":
                    need(pool, uT_copied, layer, b)
                    apart(pool)
                    g.tensor_copy(TH[:, at(b), :], UT[:]).then_inc(uT_split.sem, 1)
                    need(pool, uT_split, layer, b, 1)
                    g.tensor_tensor(TL[:, at(b), :], UT[:], as32(TH[:, at(b), :]), ALU.subtract).then_inc(uT_split.sem, 1)

            def step(t, a, m, n):
                def of(role, f, *args):
                    if role is not None:
                        f(*role, *args)

                of(n, norm_powers)
                of(t, close_attention)
                of(n, residual_base)
                of(t, split_u)
                of(m, keep_k)
                of(m, widen_v)
                of(n, keep_v)
                of(a, split_w1)

            pool.wait_ge(in_rope, 7 * 16)
            g.tensor_copy(ident_r[:], ident[:]).then_inc(vx_set, 1)
            g.memset(as32(Qst[:, :, :, 3 * HD:SL]), 0.0).then_inc(consts_set, 1)
            g.memset(as32(Kst[:, :, :, 3 * HD:SL]), 0.0).then_inc(consts_set, 1)
            pool.wait_ge(consts_set, 4)
            g.memset(as32(Kst[:, :, :, SHIFT:SHIFT + 1]), 1.0).then_inc(consts_set, 1)
            program(pool, step, lambda layer: None, lambda layer, ph: None)


_OUT = (NB, T, D)


def kernel(**inputs):
    import numpy as np
    import concourse.bacc as bacc
    from concourse.bass_utils import run_bass_kernel_spmd

    i = {k: np.asarray(v) for k, v in inputs.items()}

    def rows(a):
        return np.ascontiguousarray(np.tile(a.reshape(1, -1), (P, 1)))

    theta = (10000.0 ** (-np.arange(0, HD, 2, dtype=np.float32)[None, :] / HD)).astype(np.float32)
    freqs = np.arange(T, dtype=np.float32)[:, None] * theta
    table = np.concatenate([np.cos(freqs), np.sin(freqs)], axis=-1).astype(np.float32)
    cos, sin = table[:, ::2], table[:, 1::2]

    def spread(a):
        a = a.reshape(TT, P, HD).transpose(1, 0, 2)[:, None, :, None, :]
        return np.ascontiguousarray(np.broadcast_to(a, (P, 3, TT, H, HD)))

    a = {
        "x": i["L0_attn_a_x"],
        "w_qkv_rope": np.concatenate([i["L0_attn_a_Wq"].T, i["L0_attn_a_Wk"].T, i["L0_attn_a_Wv"].T], axis=1),
        "w_o_rope": i["L0_attn_a_Wo"].T,
        "b_qkv_rope": rows(np.concatenate([i["L0_attn_a_bq"], i["L0_attn_a_bk"], i["L0_attn_a_bv"]])),
        "b_o_rope": rows(i["L0_attn_a_bo"]),
        "w_qkv_cov": np.concatenate([i["L0_attn_b_Wq"].T, i["L0_attn_b_Wk"].T, i["L0_attn_b_Wv"].T], axis=1),
        "w_o_cov": i["L0_attn_b_Wo"].T,
        "w_qkv_ffn": i["L0_ffn_w_qkv"],
        "w_o_ffn": i["L0_ffn_w_o"],
        "b_qkv_ffn": rows(i["L0_ffn_b_qkv"]),
        "b_o_ffn": rows(i["L0_ffn_b_o"]),
        "lncols": np.stack([i["L0_ffn_ln1_w"], i["L0_ffn_ln1_b"], i["L0_ffn_ln2_w"], i["L0_ffn_ln2_b"]], axis=1),
        "w_gate": i["L0_ffn_w_gate"],
        "w1": i["L0_ffn_w1"],
        "b1c": i["L0_ffn_b1"].reshape(E * FC, P).T,
        "w2": i["L0_ffn_w2"],
        "b2": i["L0_ffn_b2"],
        "ident": np.eye(P, dtype=np.float32),
        "iota": rows(np.arange(E, dtype=np.float32)),
        "ropeA": spread(np.concatenate([cos, sin], axis=-1)),
        "ropeB": spread(np.concatenate([-sin, cos], axis=-1)),
    }
    for k in ("b_qkv_rope", "b_qkv_ffn"):
        a[k] = a[k].reshape(P, 3, D)
    nc = bacc.Bacc("TRN2", target_bir_lowering=False, num_devices=1)
    arrays, args = {}, {}
    for name, x in a.items():
        x = np.ascontiguousarray(x)
        arrays[f"in_{name}"] = x
        args[name] = nc.dram_tensor(f"in_{name}", x.shape, mybir.dt.from_np(x.dtype), kind="ExternalInput").ap()
    out = nc.dram_tensor("out_x", _OUT, F32, kind="ExternalOutput").ap()
    build(nc, args, out)
    r = run_bass_kernel_spmd(nc, [arrays], core_ids=[0])
    return r.results[0]["out_x"]
```

```python
import concourse.bass as bass
from concourse import mybir
from contextlib import ExitStack

F32 = mybir.dt.float32
F32R = mybir.dt.float32r
U32 = mybir.dt.uint32
ALU = mybir.AluOpType
ACT = mybir.ActivationFunctionType
AX = mybir.AxisListType

P = 128
D = 128
NB = 8
T = 256
TT = T // P
NT = NB * TT
H = 16
HD = D // H
SL = 32
HG = P // SL
NG = H // HG
SHIFT = 27
E = 8
FF = 512
FC = FF // P
BLK = 512
NBLK = NB * T // BLK
BT = BLK // P
EPS = 1e-5
SCALE = float(HD) ** -0.5
LAYERS = ["rope", "ffn", "cov", "ffn"]
EXP_SCALE = {"rope": SCALE, "ffn": SCALE, "cov": 1.0 / HD}


class Event:

    def __init__(self, sem, per):
        self.sem = sem
        self.per = per if isinstance(per, dict) else {k: per for k in LAYERS}

    def value(self, layer, b, k):
        per = self.per.get(LAYERS[layer], 0)
        k = per if k is None else k
        const = sum(NB * self.per.get(LAYERS[l], 0) for l in range(layer)) + k + 1
        if isinstance(b, Seq):
            return b.reg * (per * b.mul) + (const + b.off * per) if per else const
        return const + b * per


class Seq:

    def __init__(self, reg, mul, off):
        self.reg, self.mul, self.off = reg, mul, off

    @property
    def index(self):
        return self.reg * self.mul + self.off if self.off else self.reg * self.mul


def at(b):
    return b.index if isinstance(b, Seq) else b


def buf(b):
    return (b.off if isinstance(b, Seq) else b) % 2


def need(eng, event, layer, b, k=None):
    v = event.value(layer, b, k)
    if isinstance(v, int) and v <= 1:
        return
    eng.wait_ge(event.sem, v)


def build(nc, d, out):
    ctx = ExitStack()
    with ctx:
        def sb(name, shape, dt=F32):
            return ctx.enter_context(nc.sbuf_tensor(name, shape, dt))

        def sem(name):
            return ctx.enter_context(nc.semaphore(name))

        primed = []

        def event(name, per):
            primed.append(sem(name))
            return Event(primed[-1], per)

        X = sb("X", [P, NB, TT, D])
        Hs = sb("Hs", [P, NB, TT, D])
        w_qkv = {k: sb(f"w_qkv_{k}", [P, 3 * D]) for k in ("rope", "ffn", "cov")}
        w_o = {k: sb(f"w_o_{k}", [P, D]) for k in ("rope", "ffn", "cov")}
        b_qkv = {k: sb(f"b_qkv_{k}", [P, 3, D]) for k in ("rope", "ffn")}
        b_o = {k: sb(f"b_o_{k}", [P, D]) for k in ("rope", "ffn")}
        lncols = sb("lncols", [P, 4])
        w_gate = sb("w_gate", [P, E])
        w_hi = {k: sb(f"w_hi_{k}", [P, 3 * D], F32R) for k in ("rope", "ffn", "cov")}
        w_lo = {k: sb(f"w_lo_{k}", [P, 3 * D], F32R) for k in ("rope", "ffn", "cov")}
        w1h = sb("w1h", [P, E, FF], F32R)
        w1l = sb("w1l", [P, E, FF], F32R)
        b1c = sb("b1c", [P, E * FC])
        w2 = sb("w2", [P, E * FC, D])
        b2 = sb("b2", [E, D])
        ident = sb("ident", [P, P])
        ident_r = sb("ident_r", [P, P], F32R)
        iota = sb("iota", [P, E])
        ropeA = sb("ropeA", [P, 3, TT, H, HD])
        ropeB = sb("ropeB", [P, 3, TT, H, HD])
        halves = sb("halves", [P, 2 * TT])

        stats = sb("stats", [P, TT, 6])
        meanvar = sb("meanvar", [P, TT, 2])
        vareps = sb("vareps", [P, TT])
        rstd = sb("rstd", [P, TT])
        stats2 = sb("stats2", [P, TT, 6])
        meanvar2 = sb("meanvar2", [P, TT, 2])
        vareps2 = sb("vareps2", [P, TT])
        rstd2 = sb("rstd2", [P, TT])
        stats3 = sb("stats3", [P, TT, 6])
        meanvar3 = sb("meanvar3", [P, TT, 2])
        vareps3 = sb("vareps3", [P, TT])
        rstd3 = sb("rstd3", [P, TT])
        Y = sb("Y", [P, TT, D])
        Z = sb("Z", [P, TT, D])
        ZT = sb("ZT", [P, T])
        ZTh = sb("ZTh", [P, T], F32R)
        ZTl = sb("ZTl", [P, T], F32R)
        QKV = sb("QKV", [P, 3, TT, D])
        R1 = sb("R1", [P, 3, TT, H, HD])
        R2 = sb("R2", [P, 3, TT, H, HD])
        R = sb("R", [P, 3, TT, D])
        hsum = sb("hsum", [P, 2 * TT * H])
        hmean = sb("hmean", [P, 2 * TT * H])
        hsq = sb("hsq", [P, 2 * TT * H])
        Qst = sb("Qst", [P, 2, TT, H, SL], F32R)
        Kst = sb("Kst", [P, 2, TT, H, SL], F32R)
        QT = sb("QT", [P, 2, NG, T], F32R)
        KT = sb("KT", [P, 2, NG, T], F32R)
        M = sb("M", [P, 2, H, TT])
        Vmid = sb("Vmid", [P, 2, TT, D])
        Vx = sb("Vx", [P, TT, H, SL])
        Pr = sb("Pr", [P, 2, HG, TT, T])
        OT = sb("OT", [P, 2, T])
        rden = sb("rden", [P, TT, H])
        On = sb("On", [P, TT, D])
        O1 = sb("O1", [P, TT, H, HD])
        O2 = sb("O2", [P, TT, H, HD])
        Or = sb("Or", [P, TT, D])
        OnT = sb("OnT", [P, T])
        U = sb("U", [P, TT, D])
        UT = sb("UT", [P, T])
        TH = sb("TH", [P, NB, T], F32R)
        TL = sb("TL", [P, NB, T], F32R)
        G = sb("G", [P, 2, FC, BLK])
        w1raw = G[:].rearrange("p a c n -> p (a c n)").rearrange("p (e f) -> p e f", e=E)
        LG = sb("LG", [P, NB, TT * E])
        lg = LG[:].rearrange("p b (t e) -> p (b t) e", e=E)
        pe_ = sb("pe_", [P, NT, E])
        col = sb("col", [P, NT])
        col2 = sb("col2", [P, NT])
        top = sb("top", [P, NT, E])
        idx = sb("idx", [P, NT, E], U32)
        pick = sb("pick", [P, NT, E])
        WE = sb("WE", [P, NT, E])
        WT = Pr[0:E].rearrange("e b j k q -> e (b j k q)")[:, 0:NT * P].rearrange("e (n p) -> e n p", p=P)

        bankE = ctx.enter_context(nc.psum_tensor("bankE", [P, HG, TT, T], F32))
        bankO = ctx.enter_context(nc.psum_tensor("bankO", [P, 512], F32))
        bankA = ctx.enter_context(nc.psum_tensor("bankA", [P, 512], F32))
        bankB = ctx.enter_context(nc.psum_tensor("bankB", [P, 512], F32))
        bankC = ctx.enter_context(nc.psum_tensor("bankC", [P, 512], F32))
        front_bank = [bankB, bankA]

        in_x0 = sem("in_x0")
        in_x = sem("in_x")
        in_rope = sem("in_rope")
        in_rope2 = sem("in_rope2")
        in_cov = sem("in_cov")
        in_ffn = sem("in_ffn")
        in_moe = sem("in_moe")
        out_done = sem("out_done")
        primed_all = sem("primed_all")
        ffn_only = {"ffn": 1}
        norm_stats = event("norm_stats", 4)
        norm_rstd = event("norm_rstd", 2)
        normed = event("normed", 2)
        norm2_stats = event("norm2_stats", {"ffn": 4})
        norm2_rstd = event("norm2_rstd", {"ffn": 2})
        normed2 = event("normed2", {"ffn": 2})
        res_base = event("res_base", {"rope": 1, "ffn": 1})
        zT = event("zT", 1)
        zT_copied = event("zT_copied", 2)
        zT_split = event("zT_split", 1)
        proj = event("proj", 2)
        proj_copied = event("proj_copied", 2)
        roped = event("roped", {"rope": 3})
        centred = event("centred", {"cov": 5})
        k_stacked = event("k_stacked", {"rope": 2, "ffn": 2, "cov": 4})
        q_stacked = event("q_stacked", {"rope": 3, "ffn": 3, "cov": 5})
        v_mid = event("v_mid", 1)
        consts_set = sem("consts_set")
        cleared = sem("cleared")
        stackT = event("stackT", 2)
        stackT_copied = event("stackT_copied", 2)
        raw_scores = event("raw_scores", H)
        maxed = event("maxed", H)
        shifted = event("shifted", 1)
        shiftT = event("shiftT", 1)
        shiftT_copied = event("shiftT_copied", 1)
        scores = event("scores", 2 * NG)
        exped = event("exped", 2 * NG)
        pv = event("pv", NG)
        pv_copied = event("pv_copied", 2)
        v_ready = event("v_ready", 2)
        outT = event("outT", 1)
        divided = event("divided", 3)
        unroped = event("unroped", {"rope": 3})
        onT = event("onT", 1)
        onT_copied = event("onT_copied", 1)
        wo = event("wo", 1)
        res = event("res", 1)
        w1_split = event("w1_split", {"rope": 2})
        xh = event("xh", ffn_only)
        norm3_stats = event("norm3_stats", {"ffn": 4})
        norm3_rstd = event("norm3_rstd", {"ffn": 2})
        normed3 = event("normed3", {"ffn": 2})
        uT = event("uT", ffn_only)
        uT_copied = event("uT_copied", {"ffn": 2})
        uT_split = event("uT_split", ffn_only)
        gate = event("gate", ffn_only)
        gate_copied = event("gate_copied", ffn_only)
        waits_met = sem("waits_met")
        vx_set = sem("vx_set")
        w_split = sem("w_split")
        gated = sem("gated")
        gate_exp = sem("gate_exp")
        hid = sem("hid")
        hid_act = sem("hid_act")
        expert = sem("expert")
        mixed = sem("mixed")
        weT = sem("weT")
        weT_copied = sem("weT_copied")
        b2mix = sem("b2mix")
        b2_added = sem("b2_added")
        primed += [hid_act, expert, mixed]
        NGATE = 13 + 2 * NT

        def as32(ap):
            return ap.bitcast(F32)

        def banks(b):
            return front_bank[b % 2]

        def apart(eng):
            eng.sem_inc(waits_met, 1)

        block = ctx.enter_context(nc.Block())

        def program(eng, step, before_ffn, mixture):
            for ph in range(2):
                def chained(j):
                    step(*[(2 * ph + s // NB, s % NB) if 0 <= s < 2 * NB else None for s in (j - 3, j - 2, j - 1, j)])

                for half in range(2):
                    layer = 2 * ph + half
                    if half:
                        before_ffn(layer)
                    for j in range(3):
                        chained(half * NB + j)
                    with eng.Fori(0, (NB - 4) // 2) as i:
                        for u in range(2):
                            step(*[(layer, Seq(i, 2, u + r)) for r in range(4)])
                    chained(half * NB + NB - 1)
                for j in range(3):
                    chained(2 * NB + j)
                mixture(2 * ph + 1, ph)

        def first_of_all(layer, b):
            return layer == 0 and isinstance(b, int) and b == 0

        def prime(eng, events):
            for s in events:
                eng.sem_inc(s, 1)
            eng.sem_inc(primed_all, 1)

        @block.sync
        def _(sp):
            xin = d["x"].rearrange("b (t p) d -> p b t d", p=P)
            sp.dma_start(X[:, 0], xin[:, 0]).then_inc(in_x0, 16)
            prime(sp, primed[0::2])
            for b in range(1, NB):
                sp.dma_start(X[:, b], xin[:, b]).then_inc(in_x, 16)
            sp.dma_start(w_gate[:], d["w_gate"]).then_inc(in_ffn, 16)
            sp.dma_start(w_qkv["ffn"][:], d["w_qkv_ffn"]).then_inc(in_ffn, 16)
            sp.dma_start(w_o["ffn"][:], d["w_o_ffn"]).then_inc(in_ffn, 16)
            sp.dma_start(b_qkv["ffn"][:], d["b_qkv_ffn"]).then_inc(in_ffn, 16)
            sp.dma_start(b_o["ffn"][:], d["b_o_ffn"]).then_inc(in_ffn, 16)
            sp.dma_start(lncols[:], d["lncols"]).then_inc(in_ffn, 16)
            sp.dma_start(b1c[:], d["b1c"]).then_inc(in_ffn, 16)
            sp.dma_start(w1raw, d["w1"].rearrange("e p f -> p e f")).then_inc(in_ffn, 16)
            sp.dma_start(w_qkv["cov"][:], d["w_qkv_cov"]).then_inc(in_cov, 16)
            sp.dma_start(w_o["cov"][:], d["w_o_cov"]).then_inc(in_cov, 16)
            sp.dma_start(w2[:], d["w2"].rearrange("e (c p) d -> p (e c) d", p=P)).then_inc(in_moe, 16)
            sp.dma_start(b2[:], d["b2"]).then_inc(in_moe, 16)
            sp.dma_start(iota[:], d["iota"]).then_inc(in_moe, 16)
            sp.wait_ge(b2_added, 8)
            dst = out.rearrange("b (t p) d -> p b t d", p=P)
            nb = NB // NBLK
            for j in range(NBLK):
                sp.wait_ge(mixed, (NBLK + j + 1) * E * BT + 1)
                sp.dma_start(dst[:, j * nb:j * nb + nb], X[:, j * nb:j * nb + nb]).then_inc(out_done, 16)
            sp.wait_ge(out_done, NBLK * 16)

        @block.tensor
        def _(pe):
            pe.wait_ge(primed_all, 2)
            mm = nc.tensor.matmul

            def do_scores(layer, b, g, pair):
                need(pe, shiftT_copied, layer, b)
                need(pe, exped, layer, b, 2 * g + pair - 1)
                for j in (2 * pair, 2 * pair + 1):
                    rows = slice(SL * j, SL * j + SL)
                    for kc in range(TT):
                        m = mm(bankE[:, j, kc], KT[rows, buf(b), g, kc * P:kc * P + P],
                               QT[rows, buf(b), g, :],
                               start=True, stop=True)
                m.then_inc(scores.sem, 1)

            def do_pv(layer, b, g, kc):
                if kc == 0:
                    need(pe, exped, layer, b, 2 * g + 2)
                    if g == 0:
                        need(pe, pv_copied, layer, b, 0)
                        need(pe, v_ready, layer, b)
                    if g == 2:
                        need(pe, pv_copied, layer, b, 1)
                for j in range(HG):
                    rows = slice(SL * j, SL * j + SL)
                    half = g // 2
                    m = mm(bankO[rows, half * T:half * T + T], Vx[:, kc, HG * g + j, :], Pr[:, g % 2, j, kc, :],
                           start=(g % 2 == 0 and kc == 0), stop=(g % 2 == 1 and kc == TT - 1))
                if kc == TT - 1:
                    m.then_inc(pv.sem, 1)

            def do_zT(m, n):
                layer, b = n
                need(pe, normed2 if LAYERS[layer] == "ffn" else normed, layer, b)
                if m is not None:
                    need(pe, maxed, *m, 6)
                for t in range(TT):
                    k = nc.tensor.transpose(bankA[:, t * P:t * P + P], Z[:, t, :], ident[:])
                k.then_inc(zT.sem, 1)

            def do_proj(m, n, t):
                layer, b = n
                kind = LAYERS[layer]
                need(pe, zT_copied, layer, b)
                if m is not None:
                    need(pe, maxed, *m, 7 + t)
                dst = banks(t)[:, 0:3 * D]
                tok = slice(t * P, t * P + P)
                mm(dst, ZTh[:, tok], w_hi[kind][:], start=True, stop=False)
                mm(dst, ZTh[:, tok], w_lo[kind][:], start=False, stop=False)
                need(pe, zT_split, layer, b)
                mm(dst, ZTl[:, tok], w_hi[kind][:], start=False, stop=True).then_inc(proj.sem, 1)

            def transpose_stack(bank, src, b):
                for t in range(TT):
                    for g in range(NG):
                        k = mm(bankE[:, bank + t].rearrange("p k q -> p (k q)")[:, g * P:g * P + P],
                               src[:, buf(b), t, HG * g:HG * g + HG, :].rearrange("p h s -> p (h s)"), ident_r[:],
                               start=True, stop=True)
                return k

            def do_stackT(a, n, u):
                need(pe, q_stacked if u else k_stacked, *n)
                if a is not None:
                    need(pe, exped, *a, 2 * NG - 1 + u)
                else:
                    need(pe, stackT_copied, *n, 0)
                transpose_stack(2 * u, Qst if u else Kst, n[1]).then_inc(stackT.sem, 1)

            def do_raw(m, n, h):
                if h < 2:
                    need(pe, stackT_copied, *m)
                    need(pe, maxed, *m, h - 1)
                elif h == 7 and n is not None:
                    need(pe, zT_copied, *n)
                elif h in (8, 9) and n is not None:
                    need(pe, proj_copied, *n, h - 7)
                else:
                    need(pe, maxed, *m, h - 1)
                g, j = h // HG, h % HG
                rows = slice(SL * j, SL * j + SL)
                for t in range(TT):
                    k = mm(banks(h)[:, t * T:t * T + T], QT[rows, buf(m[1]), g, t * P:t * P + P],
                           KT[rows, buf(m[1]), g, :], start=True, stop=True)
                k.then_inc(raw_scores.sem, 1)

            def do_shiftT(a, m):
                need(pe, shifted, *a)
                need(pe, stackT_copied, *(m or a))
                need(pe, exped, *a, 0)
                transpose_stack(0, Qst, a[1]).then_inc(shiftT.sem, 1)

            def do_outT(layer, b):
                need(pe, pv_copied, layer, b)
                need(pe, res, layer, b, 0)
                need(pe, gate_copied, layer, b, 0)
                for t in range(TT):
                    for r in range(2):
                        u = 2 * t + r
                        m = nc.tensor.transpose(bankC[:, u * P:u * P + P], OT[:, r, t * P:t * P + P], ident[:])
                m.then_inc(outT.sem, 1)

            def do_onT(layer, b):
                kind = LAYERS[layer]
                need(pe, divided, layer, b)
                if kind == "rope":
                    need(pe, unroped, layer, b)
                src = Or if kind == "rope" else On
                for t in range(TT):
                    m = nc.tensor.transpose(bankC[:, t * P:t * P + P], src[:, t, :], ident[:])
                m.then_inc(onT.sem, 1)

            def do_wo(layer, b):
                kind = LAYERS[layer]
                need(pe, onT_copied, layer, b)
                if first_of_all(layer, b):
                    pe.wait_ge(in_rope2, 4 * 16)
                for t in range(TT):
                    m = mm(bankC[:, t * D:t * D + D], OnT[:, t * P:t * P + P], w_o[kind][:], start=True, stop=True)
                m.then_inc(wo.sem, 1)

            def do_uT(layer, b):
                if LAYERS[layer] == "ffn":
                    need(pe, res, layer, b)
                    need(pe, normed3, layer, b)
                    for t in range(TT):
                        m = nc.tensor.transpose(bankC[:, t * P:t * P + P], U[:, t, :], ident[:])
                    m.then_inc(uT.sem, 1)

            def do_gate(layer, b):
                if LAYERS[layer] == "ffn":
                    need(pe, uT_copied, layer, b)
                    for t in range(TT):
                        m = mm(bankC[:, t * E:t * E + E], UT[:, t * P:t * P + P], w_gate[:], start=True, stop=True)
                    m.then_inc(gate.sem, 1)

            def step(t, a, m, n):
                def of(role, f, *args):
                    if role is not None:
                        f(*role, *args)

                def raw(*hs):
                    for h in hs:
                        if m is not None:
                            do_raw(m, n, h)

                def prep(f, *args):
                    if n is not None:
                        f(m, n, *args)

                raw(0)
                of(t, do_pv, 2, 1)
                raw(1)
                raw(2)
                if a is not None:
                    do_shiftT(a, m)
                of(t, do_pv, 3, 0)
                raw(3)
                of(a, do_scores, 0, 0)
                raw(4)
                raw(5)
                of(t, do_pv, 3, 1)
                of(a, do_scores, 0, 1)
                of(t, do_outT)
                raw(6)
                prep(do_zT)
                of(a, do_scores, 1, 0)
                raw(7)
                of(a, do_scores, 1, 1)
                prep(do_proj, 0)
                prep(do_proj, 1)
                of(a, do_pv, 0, 0)
                raw(8)
                of(a, do_pv, 0, 1)
                raw(9)
                of(a, do_scores, 2, 0)
                raw(10)
                of(t, do_onT)
                of(a, do_pv, 1, 0)
                of(a, do_scores, 2, 1)
                raw(11)
                of(t, do_wo)
                raw(12)
                of(a, do_pv, 1, 1)
                of(a, do_scores, 3, 0)
                raw(13)
                of(a, do_scores, 3, 1)
                raw(14)
                of(a, do_pv, 2, 0)
                if n is not None:
                    do_stackT(a, n, 0)
                raw(15)
                of(t, do_uT)
                if n is not None:
                    do_stackT(a, n, 1)
                of(t, do_gate)

            def mixture(layer, ph):
                need(pe, uT_split, layer, NB - 1)
                need(pe, exped, layer, NB - 1)
                if ph == 0:
                    pe.wait_ge(in_moe, 3 * 16)
                need(pe, w1_split, layer, 0, 0)

                def hidden(j, e):
                    for c in range(FC):
                        base = ph * NBLK * E * FC + e * FC + c - FC + 1
                        v = j * (E * FC) + (base + 1)
                        if e or ph:
                            pe.wait_ge(hid_act, v)
                        else:
                            pe.wait_ge(hid_act, j * (E * FC) + 1)
                        w = slice(c * P, c * P + P)
                        n = (e * FC + c) % 4
                        acc = bankE[:, n].rearrange("p k q -> p (k q)")
                        th = TH[:].rearrange("p b t -> p (b t)").rearrange("p (j n) -> p j n", j=NBLK)[:, j]
                        tl = TL[:].rearrange("p b t -> p (b t)").rearrange("p (j n) -> p j n", j=NBLK)[:, j]
                        mm(acc, w1h[:, e, w], th, start=True, stop=False)
                        mm(acc, w1h[:, e, w], tl, start=False, stop=False)
                        mm(acc, w1l[:, e, w], th, start=False, stop=True).then_inc(hid, 1)

                def outputs(j, e):
                    pe.wait_ge(hid_act, j * (E * FC) + (ph * NBLK * E * FC + (e + 1) * FC + 1))
                    if e >= 2 or ph:
                        pe.wait_ge(mixed, j * (E * BT) + (ph * NBLK * E * BT + (e - 1) * BT + 1))
                    else:
                        pe.wait_ge(mixed, j * (E * BT) + 1)
                    for t in range(BT):
                        for c in range(FC):
                            m = mm(banks(e)[:, t * D:t * D + D], G[:, e % 2, c, t * P:t * P + P],
                                   w2[:, e * FC + c, :], start=(c == 0), stop=(c == FC - 1))
                    m.then_inc(expert, 1)

                def blocks(lo, hi):
                    with pe.Fori(lo, hi) as j:
                        hidden(j, 0)
                        for e in range(E):
                            if e + 1 < E:
                                hidden(j, e + 1)
                            outputs(j, e)

                blocks(0, NBLK // 2)
                pe.wait_ge(gated, (ph + 1) * NGATE)
                need(pe, gate_copied, layer, NB - 1)
                need(pe, pv_copied, layer, NB - 1)
                wb = [bankC, bankO]
                for q in range(4):
                    if q >= 2:
                        pe.wait_ge(weT_copied, 4 * ph + q - 1)
                    for t in range(4):
                        m = nc.tensor.transpose(wb[q % 2][0:E, t * P:t * P + P], WE[:, 4 * q + t, :], ident[:])
                    m.then_inc(weT, 1)
                for q in range(4):
                    if q < 2:
                        pe.wait_ge(weT_copied, 4 * ph + 3 + q)
                    else:
                        pe.wait_ge(b2_added, 4 * ph + q - 1)
                    for t in range(4):
                        m = mm(wb[q % 2][:, t * D:t * D + D], WT[:, 4 * q + t, :], b2[:], start=True, stop=True)
                    m.then_inc(b2mix, 1)
                blocks(NBLK // 2, NBLK)

            def before_ffn(layer):
                pe.wait_ge(in_ffn, 8 * 16)
                pe.wait_ge(w_split, 4)

            def mixture_then(layer, ph):
                mixture(layer, ph)
                if ph == 0:
                    pe.wait_ge(in_cov, 2 * 16)
                    pe.wait_ge(w_split, 6)
                    pe.wait_ge(mixed, NBLK * E * BT + 1)
                    pe.wait_ge(b2_added, 4)
                    pe.wait_ge(hid_act, NBLK * E * FC + 1)

            pe.wait_ge(in_rope, 3 * 16)
            pe.wait_ge(vx_set, 4)
            pe.wait_ge(consts_set, 4)
            pe.wait_ge(w_split, 2)
            program(pe, step, before_ffn, mixture_then)

        @block.scalar
        def _(act):
            act.dma_start(w_qkv["rope"][:], d["w_qkv_rope"]).then_inc(in_rope, 16)
            act.dma_start(ident[:], d["ident"]).then_inc(in_rope, 16)
            act.dma_start(b_qkv["rope"][:], d["b_qkv_rope"]).then_inc(in_rope, 16)
            act.dma_start(ropeA[:], d["ropeA"]).then_inc(in_rope2, 16)
            act.dma_start(ropeB[:], d["ropeB"]).then_inc(in_rope2, 16)
            act.dma_start(w_o["rope"][:], d["w_o_rope"]).then_inc(in_rope2, 16)
            act.dma_start(b_o["rope"][:], d["b_o_rope"]).then_inc(in_rope2, 16)
            act.wait_ge(primed_all, 2)

            def copy(dst, src):
                return nc.scalar.activation(dst, src, ACT.Copy)

            def affine(layer, dst, src, c):
                if LAYERS[layer] != "ffn":
                    return copy(dst, src)
                return nc.scalar.activation(dst, src, ACT.Identity, bias=lncols[:, c + 1:c + 2],
                                            scale=lncols[:, c:c + 1])

            def do_exp(layer, b, g, pair):
                need(act, scores, layer, b, 2 * g + pair + 1)
                need(act, pv, layer, b, g - 1)
                js = slice(2 * pair, 2 * pair + 2)
                nc.scalar.activation(Pr[:, g % 2, js], bankE[:, js], ACT.Exp,
                                     scale=EXP_SCALE[LAYERS[layer]]).then_inc(exped.sem, 1)

            def do_zT(layer, b):
                need(act, zT, layer, b)
                need(act, proj, layer, b, 0)
                for dst in (ZTh, ZT):
                    affine(layer, dst[:], bankA[:, 0:T], 0).then_inc(zT_copied.sem, 1)

            def do_pv(layer, b, half):
                need(act, pv, layer, b, 2 * half + 2)
                if half == 0:
                    need(act, outT, layer, b, 0)
                copy(OT[:, half, :], bankO[:, half * T:half * T + T]).then_inc(pv_copied.sem, 1)

            def transposed(bank):
                return bankE[:, bank:bank + 2].rearrange("p t k q -> p t (k q)").rearrange("p t (g x) -> p t g x", g=NG)

            def into(dst, b):
                return dst[:, buf(b)].rearrange("p g (t x) -> p t g x", t=TT)

            def do_stackT(a, n, u):
                need(act, stackT, *n, u + 1)
                if a is not None:
                    need(act, scores, *a)
                copy(into(QT if u else KT, n[1]), transposed(2 * u)).then_inc(stackT_copied.sem, 1)

            def do_shiftT(layer, b):
                need(act, shiftT, layer, b)
                need(act, raw_scores, layer, b)
                copy(into(QT, b), transposed(0)).then_inc(shiftT_copied.sem, 1)

            def do_onT(layer, b):
                need(act, onT, layer, b)
                need(act, wo, layer, b, 0)
                copy(OnT[:], bankC[:, 0:T]).then_inc(onT_copied.sem, 1)

            def do_uT(layer, b):
                if LAYERS[layer] == "ffn":
                    need(act, uT, layer, b)
                    need(act, gate, layer, b, 0)
                    need(act, uT_split, layer, b, 0)
                    for dst in (UT[:], TH[:, at(b), :]):
                        affine(layer, dst, bankC[:, 0:T], 2).then_inc(uT_copied.sem, 1)

            def do_gate(layer, b):
                if LAYERS[layer] == "ffn":
                    need(act, gate, layer, b)
                    copy(LG[:, at(b), :], bankC[:, 0:TT * E]).then_inc(gate_copied.sem, 1)

            def step(t, a, m, n):
                def of(role, f, *args):
                    if role is not None:
                        f(*role, *args)

                of(a, do_shiftT)
                of(a, do_exp, 0, 0)
                of(t, do_pv, 1)
                of(a, do_exp, 0, 1)
                of(n, do_zT)
                of(a, do_exp, 1, 0)
                of(a, do_exp, 1, 1)
                of(t, do_onT)
                of(a, do_exp, 2, 0)
                of(a, do_exp, 2, 1)
                of(a, do_pv, 0)
                of(a, do_exp, 3, 0)
                of(a, do_exp, 3, 1)
                if n is not None:
                    do_stackT(a, n, 0)
                of(t, do_uT)
                if n is not None:
                    do_stackT(a, n, 1)
                of(t, do_gate)

            def mixture(layer, ph):
                act.wait_ge(gated, ph * NGATE + 2)
                nc.scalar.activation(pe_[:], lg, ACT.Exp).then_inc(gate_exp, 1)
                need(act, pv, layer, NB - 1)

                def blocks(lo, hi):
                    with act.Fori(lo, hi) as j:
                        for e in range(E):
                            if e >= 2 or ph:
                                act.wait_ge(expert, j * E + (ph * NBLK * E + e - 1 + 1))
                            else:
                                act.wait_ge(expert, j * E + 1)
                            for c in range(FC):
                                act.wait_ge(hid, j * (E * FC) + (ph * NBLK * E * FC + e * FC + c + 1))
                                n = (e * FC + c) % 4
                                nc.scalar.activation(G[:, e % 2, c, :], bankE[:, n].rearrange("p k q -> p (k q)"),
                                                     ACT.Gelu_apprx_tanh,
                                                     bias=b1c[:, e * FC + c:e * FC + c + 1]).then_inc(hid_act, 1)

                blocks(0, NBLK // 2)
                for q in range(4):
                    act.wait_ge(weT, 4 * ph + q + 1)
                    if q == 0 and ph:
                        act.wait_ge(b2mix, 4 * ph)
                    wb = [bankC, bankO][q % 2]
                    copy(WT[:, 4 * q:4 * q + 4, :], wb[0:E, :].rearrange("e (t p) -> e t p", t=4)).then_inc(weT_copied, 1)
                blocks(NBLK // 2, NBLK)

            program(act, step, lambda layer: act.wait_ge(in_ffn, 8 * 16), mixture)

        @block.vector
        def _(dve):
            v = nc.vector
            tt = v.tensor_tensor
            v.memset(halves[:], -0.5).then_inc(consts_set, 1)
            v.memset(Vx[:], 0.0).then_inc(vx_set, 1)
            dve.wait_ge(vx_set, 1)
            vx = Vx[:].rearrange("p t (r k j) s -> p (t r) k j s", r=2, k=2)
            for k in range(2):
                at_k = k * (HD + 1) + HD
                v.memset(vx[:, :, k, :, at_k:at_k + 1], 1.0).then_inc(vx_set, 1)
            v.memset(as32(Qst[:, :, :, :, 3 * HD:SL]), 0.0).then_inc(consts_set, 1)
            v.memset(as32(Kst[:, :, :, :, 3 * HD:SL]), 0.0).then_inc(consts_set, 1)
            dve.wait_ge(consts_set, 3)
            v.memset(as32(Kst[:, :, :, :, SHIFT:SHIFT + 1]), 1.0).then_inc(consts_set, 1)
            dve.wait_ge(in_rope, 3 * 16)
            v.tensor_copy(ident_r[:], ident[:]).then_inc(vx_set, 1)
            v.tensor_copy(w_hi["rope"][:], w_qkv["rope"][:]).then_inc(w_split, 1)
            dve.wait_ge(w_split, 1)
            tt(w_lo["rope"][:], w_qkv["rope"][:], as32(w_hi["rope"][:]), ALU.subtract).then_inc(w_split, 1)
            dve.wait_ge(primed_all, 2)

            def stats_of(layer, b, ev, src, st, mv):
                apart(dve)
                for t in range(TT):
                    v.bn_stats(st[:, t, :], src[:, t, :]).then_inc(ev.sem, 1)
                for t in range(TT):
                    need(dve, ev, layer, b, t + 1)
                    apart(dve)
                    v.bn_aggr(mv[:, t, :], st[:, t, :]).then_inc(ev.sem, 1)

            def normalise(layer, b, ev, dst, src, mv, rs):
                for t in range(TT):
                    v.tensor_scalar(dst[:, t, :], src[:, t, :], mv[:, t, 0:1], rs[:, t:t + 1],
                                    ALU.subtract, ALU.mult).then_inc(ev.sem, 1)

            def norm_in(layer, b):
                if layer == 0:
                    if isinstance(b, int) and b == 0:
                        dve.wait_ge(in_x0, 16)
                    else:
                        dve.wait_ge(in_x, (NB - 1) * 16)
                elif LAYERS[layer] != "ffn":
                    dve.wait_ge(b2_added, 4 * (layer // 2))
                else:
                    need(dve, res, layer - 1, b)
                stats_of(layer, b, norm_stats, X[:, at(b)], stats, meanvar)

            def norm_out(layer, b):
                ffn = LAYERS[layer] == "ffn"
                need(dve, norm_rstd, layer, b)
                if ffn:
                    need(dve, res_base, layer, b, 0)
                else:
                    need(dve, zT, layer, b, 0)
                normalise(layer, b, normed, Y if ffn else Z, X[:, at(b)], meanvar, rstd)
                if ffn:
                    need(dve, normed, layer, b)
                    stats_of(layer, b, norm2_stats, Y, stats2, meanvar2)

            def norm2_out(layer, b):
                if LAYERS[layer] == "ffn":
                    need(dve, norm2_rstd, layer, b)
                    need(dve, zT, layer, b, 0)
                    normalise(layer, b, normed2, Z, Y, meanvar2, rstd2)

            def split_zT(layer, b):
                need(dve, zT_copied, layer, b)
                need(dve, proj, layer, b, 0)
                tt(ZTl[:], ZT[:], as32(ZTh[:]), ALU.subtract).then_inc(zT_split.sem, 1)

            def do_proj(layer, b, t):
                kind = LAYERS[layer]
                need(dve, v_mid, layer, b, 0)
                need(dve, proj, layer, b, t + 1)
                if first_of_all(layer, b):
                    dve.wait_ge(in_rope, 3 * 16)
                src = banks(t)[:, 0:3 * D].rearrange("p (c d) -> p c d", c=3)
                if kind == "cov":
                    v.tensor_copy(QKV[:, :, t, :], src).then_inc(proj_copied.sem, 1)
                else:
                    tt(QKV[:, :, t, :], src, b_qkv[kind][:], ALU.add).then_inc(proj_copied.sem, 1)

            def heads(ap):
                return ap.rearrange("p c t (h x) -> p (c t h) x", x=HD)

            def rope_operands(ap):
                half = ap.rearrange("p n (w o) -> p n w o", o=2)
                n = ap.shape[1]
                ev = half[:, :, :, 0].unsqueeze(2).broadcast_to([P, n, 2, HD // 2])
                od = half[:, :, :, 1].unsqueeze(2).broadcast_to([P, n, 2, HD // 2])
                return ev, od

            def flat(ap):
                return ap.rearrange("p c t h (u w) -> p (c t h) u w", u=2)

            def rope(layer, b, part):
                ev, od = rope_operands(heads(QKV[:]))
                if part == 0:
                    need(dve, proj_copied, layer, b)
                    if first_of_all(layer, b):
                        dve.wait_ge(in_rope2, 4 * 16)
                    tt(flat(R1[:]), ev, flat(ropeA[:]), ALU.mult).then_inc(roped.sem, 1)
                elif part == 1:
                    tt(flat(R2[:]), od, flat(ropeB[:]), ALU.mult).then_inc(roped.sem, 1)
                else:
                    need(dve, roped, layer, b, 2)
                    tt(heads(R[:]), R1[:].rearrange("p c t h x -> p (c t h) x"),
                       R2[:].rearrange("p c t h x -> p (c t h) x"), ALU.add).then_inc(roped.sem, 1)

            def centre(layer, b, part):
                n = 2 * TT * H
                qk = heads(QKV[:, 0:2])
                dst = heads(R[:, 0:2])
                sq = R1[:, 0:2].rearrange("p c t h x -> p (c t h) x")
                if part == 0:
                    need(dve, proj_copied, layer, b)
                    v.tensor_reduce(hsum[:], qk, AX.X, ALU.add).then_inc(centred.sem, 1)
                    need(dve, centred, layer, b, 1)
                    v.tensor_scalar(hmean[:], hsum[:], 1.0 / HD, None, ALU.mult).then_inc(centred.sem, 1)
                elif part == 1:
                    need(dve, centred, layer, b, 2)
                    tt(dst, qk, hmean[:].unsqueeze(2).broadcast_to([P, n, HD]), ALU.subtract).then_inc(centred.sem, 1)
                else:
                    need(dve, centred, layer, b, 3)
                    tt(sq, dst, dst, ALU.mult).then_inc(centred.sem, 1)
                    need(dve, centred, layer, b, 4)
                    v.tensor_reduce(hsq[:], sq, AX.X, ALU.add).then_inc(centred.sem, 1)

            def turn(layer, b, part):
                if LAYERS[layer] == "rope":
                    rope(layer, b, part)
                elif LAYERS[layer] == "cov":
                    centre(layer, b, part)

            def stack_operand(layer, c):
                kind = LAYERS[layer]
                src = QKV if kind == "ffn" else R
                return src[:, c].rearrange("p t (h x) -> p (t h) x", x=HD)

            STH = TT * H
            INV = 1.0 / (HD - 1)

            def twice(ap):
                return ap.unsqueeze(2).broadcast_to([P, STH, 2, HD])

            cleared_count = [0]

            def clear(stack, layer, b):
                if layer == 3 and isinstance(b, int) and b < 2:
                    v.memset(as32(stack[:, :, 3 * HD:SHIFT]), 0.0).then_inc(cleared, 1)
                    cleared_count[0] += 1
                    dve.wait_ge(cleared, cleared_count[0])

            def stack_k(a, n, part):
                layer, b = n
                kind = LAYERS[layer]
                k = stack_operand(layer, 1)
                ks = Kst[:, buf(b)].rearrange("p t h s -> p (t h) s")
                hk = hsq[:, STH:2 * STH].unsqueeze(2)
                if part == 0:
                    need(dve, {"ffn": proj_copied, "rope": roped, "cov": centred}[kind], layer, b)
                    if a is not None:
                        need(dve, stackT, *a)
                    if first_of_all(layer, b):
                        dve.wait_ge(consts_set, 4)
                    clear(ks, layer, b)
                    k_hi = ks[:, :, 0:4 * HD].rearrange("p n (r y) -> p n r y", r=2)[:, :, :, 0:HD]
                    v.tensor_copy(k_hi, twice(k)).then_inc(k_stacked.sem, 1)
                    if kind == "cov":
                        v.tensor_scalar(ks[:, :, 24:28].rearrange("p n (r y) -> p n r y", y=2)[:, :, :, 0],
                                        hk.broadcast_to([P, STH, 2]), INV, None, ALU.mult).then_inc(k_stacked.sem, 1)
                else:
                    need(dve, k_stacked, layer, b, 2 if kind == "cov" else 1)
                    tt(ks[:, :, HD:2 * HD], k, as32(ks[:, :, 0:HD]), ALU.subtract).then_inc(k_stacked.sem, 1)
                    if kind == "cov":
                        v.scalar_tensor_tensor(ks[:, :, 25:26], hk, INV, as32(ks[:, :, 24:25]),
                                               ALU.mult, ALU.subtract).then_inc(k_stacked.sem, 1)

            def stack_q(a, n):
                layer, b = n
                kind = LAYERS[layer]
                q = stack_operand(layer, 0)
                qs = Qst[:, buf(b)].rearrange("p t h s -> p (t h) s")
                hq = hsq[:, 0:STH].unsqueeze(2)
                need(dve, {"ffn": proj_copied, "rope": roped, "cov": centred}[kind], layer, b)
                if a is not None:
                    need(dve, shiftT, *a)
                clear(qs, layer, b)
                v.tensor_copy(qs[:, :, 0:2 * HD].rearrange("p n (r x) -> p n r x", r=2),
                              twice(q)).then_inc(q_stacked.sem, 1)
                v.memset(as32(qs[:, :, SHIFT:SHIFT + 1]), 0.0).then_inc(q_stacked.sem, 1)
                if kind == "cov":
                    v.tensor_scalar(qs[:, :, 24:26], hq.broadcast_to([P, STH, 2]), INV, None,
                                    ALU.mult).then_inc(q_stacked.sem, 1)
                need(dve, q_stacked, layer, b, 3 if kind == "cov" else 1)
                tt(qs[:, :, 2 * HD:3 * HD], q, as32(qs[:, :, 0:HD]), ALU.subtract).then_inc(q_stacked.sem, 1)
                if kind == "cov":
                    v.scalar_tensor_tensor(qs[:, :, 26:27], hq, INV, as32(qs[:, :, 24:25]),
                                           ALU.mult, ALU.subtract).then_inc(q_stacked.sem, 1)

            def do_max(layer, b, h):
                need(dve, raw_scores, layer, b, h + 1)
                v.tensor_reduce(M[:, buf(b), h, :], banks(h)[:].rearrange("p (t k) -> p t k", t=TT),
                                AX.X, ALU.max).then_inc(maxed.sem, 1)

            def shift(layer, b):
                need(dve, maxed, layer, b)
                need(dve, stackT, layer, b)
                v.tensor_scalar(Qst[:, buf(b), :, :, SHIFT], M[:, buf(b)].rearrange("p h t -> p t h"), -1.0, None,
                                ALU.mult).then_inc(shifted.sem, 1)

            def divide(layer, b):
                need(dve, outT, layer, b)
                need(dve, onT, layer, b, 0)
                o = bankC[:].rearrange("p (u j s) -> p u j s", u=2 * TT, s=SL)
                den = bankC[:].rearrange("p (u j s) -> p u s j", u=2 * TT, s=SL)[:, :, HD:2 * HD + 2:HD + 1, :]
                rd = rden[:].rearrange("p t (r k j) -> p (t r) k j", r=2, k=2)
                on = On[:].rearrange("p t (r k j x) -> p (t r) k j x", r=2, k=2, x=HD)
                v.reciprocal(rd, den).then_inc(divided.sem, 1)
                need(dve, divided, layer, b, 1)
                for k in range(2):
                    at_k = k * (HD + 1)
                    tt(on[:, :, k], o[:, :, :, at_k:at_k + HD],
                       rd[:, :, k].unsqueeze(3).broadcast_to([P, 2 * TT, HG, HD]), ALU.mult).then_inc(divided.sem, 1)

            def unrope(layer, b):
                need(dve, divided, layer, b)
                ev, od = rope_operands(On[:].rearrange("p t (h x) -> p (t h) x", x=HD))
                f = lambda ap: ap.rearrange("p t h (u w) -> p (t h) u w", u=2)
                tt(f(O1[:]), ev, f(ropeA[:, 0]), ALU.mult).then_inc(unroped.sem, 1)
                tt(f(O2[:]), od, f(ropeB[:, 0]), ALU.mult).then_inc(unroped.sem, 1)
                need(dve, unroped, layer, b, 2)
                need(dve, onT, layer, b, 0)
                v.scalar_tensor_tensor(Or[:].rearrange("p t d -> p (t d)"), O1[:].rearrange("p t h x -> p (t h x)"),
                                       -1.0, O2[:].rearrange("p t h x -> p (t h x)"),
                                       ALU.mult, ALU.subtract).then_inc(unroped.sem, 1)

            def residual(layer, b):
                kind = LAYERS[layer]
                need(dve, wo, layer, b)
                if kind != "cov":
                    need(dve, res_base, layer, b)
                dst = Hs if kind == "ffn" else X
                tt(dst[:, at(b)], bankC[:, 0:T].rearrange("p (t d) -> p t d", t=TT), dst[:, at(b)],
                   ALU.add).then_inc(res.sem, 1)

            def norm3_in(layer, b):
                if LAYERS[layer] == "ffn":
                    need(dve, res, layer, b)
                    stats_of(layer, b, norm3_stats, Hs[:, at(b)], stats3, meanvar3)

            def norm3_out(layer, b):
                if LAYERS[layer] == "ffn":
                    need(dve, norm3_rstd, layer, b)
                    need(dve, uT, layer, b, 0)
                    normalise(layer, b, normed3, U, Hs[:, at(b)], meanvar3, rstd3)

            def unrope_if(layer, b):
                if LAYERS[layer] == "rope":
                    unrope(layer, b)

            def step(t, a, m, n):
                def of(role, f, *args):
                    if role is not None:
                        f(*role, *args)

                def maxima(*hs):
                    for h in hs:
                        of(m, do_max, h)

                of(a, shift)
                maxima(0)
                of(n, norm_in)
                maxima(1, 2)
                of(n, norm_out)
                maxima(3, 4)
                of(n, norm2_out)
                maxima(5, 6)
                of(n, split_zT)
                of(t, divide)
                maxima(7)
                of(n, do_proj, 0)
                of(n, do_proj, 1)
                maxima(8)
                of(t, unrope_if)
                maxima(9)
                of(n, turn, 0)
                maxima(10)
                of(n, turn, 1)
                maxima(11)
                of(n, turn, 2)
                if n is not None:
                    stack_k(a, n, 0)
                maxima(12)
                of(t, residual)
                if n is not None:
                    stack_k(a, n, 1)
                of(t, norm3_in)
                maxima(13)
                if n is not None:
                    stack_q(a, n)
                of(t, norm3_out)
                maxima(14, 15)

            def mixture(layer, ph):
                done = [ph * NGATE]

                def then(ins):
                    ins.then_inc(gated, 1)
                    done[0] += 1
                    dve.wait_ge(gated, done[0])

                def across(c):
                    return c.unsqueeze(2).broadcast_to([P, NT, E])

                if ph == 0:
                    dve.wait_ge(in_moe, 3 * 16)
                need(dve, gate_copied, layer, NB - 1)
                then(v.tensor_reduce(col[:], lg, AX.X, ALU.max))
                then(tt(lg, lg, across(col[:]), ALU.subtract))
                dve.wait_ge(gate_exp, ph + 1)
                then(v.tensor_reduce(col[:], pe_[:], AX.X, ALU.add))
                then(v.reciprocal(col2[:], col[:]))
                then(tt(pe_[:], pe_[:], across(col2[:]), ALU.mult))
                for t in range(NT):
                    then(v.max(top[:, t, :], pe_[:, t, :]))
                for t in range(NT):
                    then(v.max_index(idx[:, t, :], top[:, t, :], pe_[:, t, :]))
                then(tt(col[:], top[:, :, 0], top[:, :, 1], ALU.add))
                then(v.reciprocal(col2[:], col[:]))
                then(tt(top[:, :, 0:2], top[:, :, 0:2], col2[:].unsqueeze(2).broadcast_to([P, NT, 2]), ALU.mult))
                io = iota[:].unsqueeze(1).broadcast_to([P, NT, E])
                then(tt(pick[:], io, across(idx[:, :, 0]), ALU.is_equal))
                if ph:
                    dve.wait_ge(weT, 4 * ph)
                then(tt(WE[:], pick[:], across(top[:, :, 0]), ALU.mult))
                then(tt(pick[:], io, across(idx[:, :, 1]), ALU.is_equal))
                then(tt(pick[:], pick[:], across(top[:, :, 1]), ALU.mult))
                then(tt(WE[:], WE[:], pick[:], ALU.add))

                need(dve, xh, layer, NB - 1)
                xt = X[:].rearrange("p b t d -> p (b t) d").rearrange("p (j t) d -> p j t d", j=NBLK)
                we = WE[:].rearrange("p (j t) e -> p j t e", j=NBLK)

                def blocks(lo, hi):
                    with dve.Fori(lo, hi) as j:
                        for e in range(E):
                            dve.wait_ge(expert, j * E + (ph * NBLK * E + e + 1 + 1))
                            for t in range(BT):
                                if e or ph:
                                    dve.wait_ge(mixed, j * (E * BT) + (ph * NBLK * E * BT + (e - 1) * BT + t + 1 + 1))
                                v.scalar_tensor_tensor(xt[:, j, t, :], banks(e)[:, t * D:t * D + D],
                                                       we[:, j, t, e:e + 1], xt[:, j, t, :],
                                                       ALU.mult, ALU.add).then_inc(mixed, 1)

                blocks(0, NBLK // 2)
                dve.wait_ge(mixed, ph * NBLK * E * BT + NBLK // 2 * E * BT + 1)
                for q in range(4):
                    dve.wait_ge(b2mix, 4 * ph + q + 1)
                    xq = X[:].rearrange("p b t d -> p (b t) d")[:, 4 * q:4 * q + 4, :]
                    tt(xq, [bankC, bankO][q % 2][:].rearrange("p (t d) -> p t d", t=4), xq,
                       ALU.add).then_inc(b2_added, 1)
                dve.wait_ge(b2_added, 4 * ph + 4)
                blocks(NBLK // 2, NBLK)
                dve.wait_ge(mixed, (ph + 1) * NBLK * E * BT + 1)


            program(dve, step, lambda layer: dve.wait_ge(in_ffn, 8 * 16), mixture)

        @block.gpsimd
        def _(pool):
            prime(pool, primed[1::2])
            pool.wait_ge(primed_all, 2)
            g = nc.gpsimd
            vx = Vx[:].rearrange("p t (r k j) s -> p (t r) k j s", r=2, k=2)
            pool.wait_ge(consts_set, 1)
            pool.wait_ge(vx_set, 3)

            def power(layer, b, stats_ev, ev, mv, ve, rs, applied):
                need(pool, stats_ev, layer, b)
                need(pool, applied, layer, b, 0)
                apart(pool)
                g.tensor_scalar(ve[:], mv[:, :, 1], EPS, None, ALU.add).then_inc(ev.sem, 1)
                need(pool, ev, layer, b, 1)
                g.tensor_tensor(rs[:], ve[:], halves[:, 0:TT], ALU.pow).then_inc(ev.sem, 1)

            def norm_powers(layer, b):
                power(layer, b, norm_stats, norm_rstd, meanvar, vareps, rstd, normed)
                if LAYERS[layer] == "ffn":
                    power(layer, b, norm2_stats, norm2_rstd, meanvar2, vareps2, rstd2, normed2)

            def residual_base(layer, b):
                kind = LAYERS[layer]
                if kind != "cov":
                    need(pool, normed, layer, b)
                    if first_of_all(layer, b):
                        pool.wait_ge(in_rope2, 4 * 16)
                    src = Y[:] if kind == "ffn" else X[:, at(b)]
                    dst = Hs[:, at(b)] if kind == "ffn" else X[:, at(b)]
                    g.tensor_tensor(dst, src, b_o[kind][:].unsqueeze(1).broadcast_to([P, TT, D]),
                                    ALU.add).then_inc(res_base.sem, 1)

            def widen_v(layer, b):
                need(pool, v_mid, layer, b)
                need(pool, pv, layer, b, 0)
                vm = Vmid[:, buf(b)].rearrange("p t (r k j x) -> p (t r) k j x", r=2, k=2, x=HD)
                apart(pool)
                for k in range(2):
                    at_k = k * (HD + 1)
                    g.tensor_copy(vx[:, :, k, :, at_k:at_k + HD], vm[:, :, k]).then_inc(v_ready.sem, 1)

            def keep_v(a, n):
                layer, b = n
                kind = LAYERS[layer]
                need(pool, roped if kind == "rope" else proj_copied, layer, b)
                if a is not None:
                    need(pool, v_ready, *a)
                apart(pool)
                src = R if kind == "rope" else QKV
                g.tensor_copy(Vmid[:, buf(b)], src[:, 2]).then_inc(v_mid.sem, 1)

            def split_w1(layer, b):
                if LAYERS[layer] != "rope":
                    return
                e = at(b)
                pool.wait_ge(in_ffn, 8 * 16)
                need(pool, w1_split, layer, b, 0)
                apart(pool)
                g.tensor_copy(w1h[:, e, :], w1raw[:, e, :]).then_inc(w1_split.sem, 1)
                need(pool, w1_split, layer, b, 1)
                g.tensor_tensor(w1l[:, e, :], w1raw[:, e, :], as32(w1h[:, e, :]), ALU.subtract).then_inc(w1_split.sem, 1)

            def close_attention(layer, b):
                if LAYERS[layer] == "ffn":
                    need(pool, res, layer, b)
                    power(layer, b, norm3_stats, norm3_rstd, meanvar3, vareps3, rstd3, normed3)
                    g.tensor_tensor(X[:, at(b)], X[:, at(b)], Hs[:, at(b)], ALU.add).then_inc(xh.sem, 1)

            def split_u(layer, b):
                if LAYERS[layer] == "ffn":
                    need(pool, uT_copied, layer, b)
                    g.tensor_tensor(TL[:, at(b), :], UT[:], as32(TH[:, at(b), :]), ALU.subtract).then_inc(uT_split.sem, 1)

            w_splits = [2]

            def split_w(kind):
                g.tensor_copy(w_hi[kind][:], w_qkv[kind][:]).then_inc(w_split, 1)
                w_splits[0] += 1
                pool.wait_ge(w_split, w_splits[0])
                g.tensor_tensor(w_lo[kind][:], w_qkv[kind][:], as32(w_hi[kind][:]), ALU.subtract).then_inc(w_split, 1)
                w_splits[0] += 1

            def step(t, a, m, n):
                def of(role, f, *args):
                    if role is not None:
                        f(*role, *args)

                of(n, norm_powers)
                of(a, widen_v)
                of(n, residual_base)
                if n is not None:
                    keep_v(a, n)
                of(t, close_attention)
                of(t, split_u)
                of(a, split_w1)

            pool.wait_ge(in_rope, 3 * 16)
            def before_ffn(layer):
                if layer == 1:
                    pool.wait_ge(in_ffn, 8 * 16)
                    split_w("ffn")
                    pool.wait_ge(in_cov, 2 * 16)
                    split_w("cov")

            program(pool, step, before_ffn, lambda layer, ph: None)


_OUT = (NB, T, D)


def kernel(**inputs):
    import numpy as np
    import concourse.bacc as bacc
    from concourse.bass_utils import run_bass_kernel_spmd

    i = {k: np.asarray(v) for k, v in inputs.items()}

    def rows(a):
        return np.ascontiguousarray(np.tile(a.reshape(1, -1), (P, 1)))

    theta = (10000.0 ** (-np.arange(0, HD, 2, dtype=np.float32)[None, :] / HD)).astype(np.float32)
    freqs = np.arange(T, dtype=np.float32)[:, None] * theta
    table = np.concatenate([np.cos(freqs), np.sin(freqs)], axis=-1).astype(np.float32)
    cos, sin = table[:, ::2], table[:, 1::2]

    def spread(a):
        a = a.reshape(TT, P, HD).transpose(1, 0, 2)[:, None, :, None, :]
        return np.ascontiguousarray(np.broadcast_to(a, (P, 3, TT, H, HD)))

    a = {
        "x": i["L0_attn_a_x"],
        "w_qkv_rope": np.concatenate([i["L0_attn_a_Wq"].T, i["L0_attn_a_Wk"].T, i["L0_attn_a_Wv"].T], axis=1),
        "w_o_rope": i["L0_attn_a_Wo"].T,
        "b_qkv_rope": rows(np.concatenate([i["L0_attn_a_bq"], i["L0_attn_a_bk"], i["L0_attn_a_bv"]])),
        "b_o_rope": rows(i["L0_attn_a_bo"]),
        "w_qkv_cov": np.concatenate([i["L0_attn_b_Wq"].T, i["L0_attn_b_Wk"].T, i["L0_attn_b_Wv"].T], axis=1),
        "w_o_cov": i["L0_attn_b_Wo"].T,
        "w_qkv_ffn": i["L0_ffn_w_qkv"],
        "w_o_ffn": i["L0_ffn_w_o"],
        "b_qkv_ffn": rows(i["L0_ffn_b_qkv"]),
        "b_o_ffn": rows(i["L0_ffn_b_o"]),
        "lncols": np.stack([i["L0_ffn_ln1_w"], i["L0_ffn_ln1_b"], i["L0_ffn_ln2_w"], i["L0_ffn_ln2_b"]], axis=1),
        "w_gate": i["L0_ffn_w_gate"],
        "w1": i["L0_ffn_w1"],
        "b1c": i["L0_ffn_b1"].reshape(E * FC, P).T,
        "w2": i["L0_ffn_w2"],
        "b2": i["L0_ffn_b2"],
        "ident": np.eye(P, dtype=np.float32),
        "iota": rows(np.arange(E, dtype=np.float32)),
        "ropeA": spread(np.concatenate([cos, sin], axis=-1)),
        "ropeB": spread(np.concatenate([-sin, cos], axis=-1)),
    }
    for k in ("b_qkv_rope", "b_qkv_ffn"):
        a[k] = a[k].reshape(P, 3, D)
    nc = bacc.Bacc("TRN2", target_bir_lowering=False, num_devices=1)
    arrays, args = {}, {}
    for name, x in a.items():
        x = np.ascontiguousarray(x)
        arrays[f"in_{name}"] = x
        args[name] = nc.dram_tensor(f"in_{name}", x.shape, mybir.dt.from_np(x.dtype), kind="ExternalInput").ap()
    out = nc.dram_tensor("out_x", _OUT, F32, kind="ExternalOutput").ap()
    build(nc, args, out)
    r = run_bass_kernel_spmd(nc, [arrays], core_ids=[0])
    return r.results[0]["out_x"]
```
